# Optimizing a Trainium2 kernel written in Bass

```python
import numpy as np
import jax
import jax.numpy as jnp

def _softmax(x, axis=-1):
    return jax.nn.softmax(x, axis=axis)

def _gelu(x):
    return jax.nn.gelu(x, approximate=True)

def _silu(x):
    return jax.nn.silu(x)

def _sigmoid(x):
    return jax.nn.sigmoid(x)

def _layernorm(x, axis=-1, eps=1e-05):
    m = jnp.mean(x, axis=axis, keepdims=True)
    v = jnp.var(x, axis=axis, keepdims=True)
    return (x - m) / jnp.sqrt(v + eps)

def _scatter_add(tgt, idx, src, axis=0):
    return tgt.at[idx].add(src)

def _segment_sum(src, seg, n):
    return jax.ops.segment_sum(src, seg, n)
kernel_name = 'mk_prb_d1_jaxref_r8_d171fb'

def setup_inputs(seed: int=0):
    np.random.seed(seed)
    _w = jnp.asarray

    def _L0_attn_setup():
        import jax, jax.numpy as jnp
        import numpy as np
        D_MODEL = 128
        N_HEADS = 16
        N_KV = 4
        HEAD_DIM = D_MODEL // N_HEADS
        SEQ = 256
        BATCH = 2
        CAP = 50.0
        EPS = 1e-05
        THETA = 10000.0

        def _rms_norm(x, eps=EPS):
            return x * jax.lax.rsqrt(jnp.mean(jnp.square(x), axis=-1, keepdims=True) + eps)

        def _rope_cos_sin(seq_len, head_dim, theta=THETA):
            inv_freq = 1.0 / theta ** (jnp.arange(0, head_dim, 2, dtype=jnp.float32) / head_dim)
            freqs = jnp.arange(seq_len, dtype=jnp.float32)[:, None] * inv_freq[None, :]
            return (jnp.cos(freqs)[None, :, None, :], jnp.sin(freqs)[None, :, None, :])

        def _apply_rope(x, cos, sin):
            d = x.shape[-1] // 2
            x1, x2 = (x[..., :d], x[..., d:])
            return jnp.concatenate([x1 * cos - x2 * sin, x2 * cos + x1 * sin], axis=-1).astype(x.dtype)
        key = jax.random.key(seed)
        ks = jax.random.split(key, 5)
        s = 0.02
        return {'x': jax.random.normal(ks[0], (BATCH, SEQ, D_MODEL), dtype=jnp.float32), 'w_q': jax.random.normal(ks[1], (D_MODEL, N_HEADS * HEAD_DIM), dtype=jnp.float32) * s, 'w_k': jax.random.normal(ks[2], (D_MODEL, N_KV * HEAD_DIM), dtype=jnp.float32) * s, 'w_v': jax.random.normal(ks[3], (D_MODEL, N_KV * HEAD_DIM), dtype=jnp.float32) * s, 'w_o': jax.random.normal(ks[4], (N_HEADS * HEAD_DIM, D_MODEL), dtype=jnp.float32) * s}
    _L0_attn_in = _L0_attn_setup()

    def _L0_ffn_setup():
        import jax, jax.numpy as jnp
        import numpy as np
        B, S, D, F, E = (2, 256, 128, 512, 8)
        LN_EPS = 1e-05

        def _layer_norm(x, gamma, beta):
            mu = jnp.mean(x, axis=-1, keepdims=True)
            var = jnp.mean(jnp.square(x - mu), axis=-1, keepdims=True)
            return (x - mu) * jax.lax.rsqrt(var + LN_EPS) * gamma + beta
        key = jax.random.key(seed)
        ks = jax.random.split(key, 8)

        def xavier(k, shape):
            fan_in, fan_out = (shape[-1], shape[-2])
            a = jnp.sqrt(6.0 / (fan_in + fan_out))
            return jax.random.uniform(k, shape, jnp.float32, -a, a)
        return {'tgt': jax.random.normal(ks[0], (B, S, D), jnp.float32), 'Wr': xavier(ks[1], (E, D)), 'br': jnp.zeros((E,), jnp.float32), 'W1': xavier(ks[2], (E, F, D)), 'b1': jnp.zeros((E, F), jnp.float32), 'W2': xavier(ks[3], (E, D, F)), 'b2': jnp.zeros((E, D), jnp.float32), 'gamma': jnp.ones((D,), jnp.float32), 'beta': jnp.zeros((D,), jnp.float32)}
    _L0_ffn_in = _L0_ffn_setup()
    _d = {'L0_attn_x': _L0_attn_in['x'], 'L0_attn_w_q': _L0_attn_in['w_q'], 'L0_attn_w_k': _L0_attn_in['w_k'], 'L0_attn_w_v': _L0_attn_in['w_v'], 'L0_attn_w_o': _L0_attn_in['w_o'], 'L0_ffn_Wr': _L0_ffn_in['Wr'], 'L0_ffn_br': _L0_ffn_in['br'], 'L0_ffn_W1': _L0_ffn_in['W1'], 'L0_ffn_b1': _L0_ffn_in['b1'], 'L0_ffn_W2': _L0_ffn_in['W2'], 'L0_ffn_b2': _L0_ffn_in['b2'], 'L0_ffn_gamma': _L0_ffn_in['gamma'], 'L0_ffn_beta': _L0_ffn_in['beta']}
    _x0 = _d['L0_attn_x']
    _d['L0_attn_x'] = jax.random.normal(jax.random.fold_in(jax.random.key(seed), 1), (16, 512, 128), dtype=_x0.dtype)
    del _x0
    return _d

def reference(L0_attn_x, L0_attn_w_q, L0_attn_w_k, L0_attn_w_v, L0_attn_w_o, L0_ffn_Wr, L0_ffn_br, L0_ffn_W1, L0_ffn_b1, L0_ffn_W2, L0_ffn_b2, L0_ffn_gamma, L0_ffn_beta):

    def _L0_attn_ref(x, w_q, w_k, w_v, w_o):
        import jax, jax.numpy as jnp
        import numpy as np
        D_MODEL = 128
        N_HEADS = 16
        N_KV = 4
        HEAD_DIM = D_MODEL // N_HEADS
        SEQ = 256
        BATCH = 2
        CAP = 50.0
        EPS = 1e-05
        THETA = 10000.0

        def _rms_norm(x, eps=EPS):
            return x * jax.lax.rsqrt(jnp.mean(jnp.square(x), axis=-1, keepdims=True) + eps)

        def _rope_cos_sin(seq_len, head_dim, theta=THETA):
            inv_freq = 1.0 / theta ** (jnp.arange(0, head_dim, 2, dtype=jnp.float32) / head_dim)
            freqs = jnp.arange(seq_len, dtype=jnp.float32)[:, None] * inv_freq[None, :]
            return (jnp.cos(freqs)[None, :, None, :], jnp.sin(freqs)[None, :, None, :])

        def _apply_rope(x, cos, sin):
            d = x.shape[-1] // 2
            x1, x2 = (x[..., :d], x[..., d:])
            return jnp.concatenate([x1 * cos - x2 * sin, x2 * cos + x1 * sin], axis=-1).astype(x.dtype)
        B, S, _ = x.shape
        q = (x @ w_q).reshape(B, S, N_HEADS, HEAD_DIM)
        k = (x @ w_k).reshape(B, S, N_KV, HEAD_DIM)
        v = (x @ w_v).reshape(B, S, N_KV, HEAD_DIM)
        q = _rms_norm(q)
        k = _rms_norm(k)
        cos, sin = _rope_cos_sin(S, HEAD_DIM)
        q = _apply_rope(q, cos, sin)
        k = _apply_rope(k, cos, sin)
        rep = N_HEADS // N_KV
        k = jnp.repeat(k, rep, axis=2)
        v = jnp.repeat(v, rep, axis=2)
        scores = jnp.einsum('bqhd,bkhd->bhqk', q, k) / np.sqrt(HEAD_DIM).astype(np.float32)
        scores = jnp.tanh(scores.astype(jnp.float32) / CAP) * CAP
        causal = jnp.tril(jnp.ones((S, S), dtype=bool))
        scores = jnp.where(causal[None, None], scores, -jnp.inf)
        probs = jax.nn.softmax(scores, axis=-1)
        y = jnp.einsum('bhqk,bkhd->bqhd', probs, v).reshape(B, S, N_HEADS * HEAD_DIM)
        return y @ w_o

    def _L0_ffn_ref(tgt, Wr, br, W1, b1, W2, b2, gamma, beta):
        import jax, jax.numpy as jnp
        import numpy as np
        B, S, D, F, E = (2, 256, 128, 512, 8)
        LN_EPS = 1e-05

        def _layer_norm(x, gamma, beta):
            mu = jnp.mean(x, axis=-1, keepdims=True)
            var = jnp.mean(jnp.square(x - mu), axis=-1, keepdims=True)
            return (x - mu) * jax.lax.rsqrt(var + LN_EPS) * gamma + beta
        logits = jnp.einsum('bsd,ed->bse', tgt, Wr) + br
        top_v, top_i = jax.lax.top_k(logits, 2)
        top_w = jax.nn.softmax(top_v, axis=-1)
        n_exp = logits.shape[-1]
        router_w = jnp.sum(jax.nn.one_hot(top_i, n_exp, dtype=top_w.dtype) * top_w[..., None], axis=-2)
        h = jnp.einsum('bsd,efd->bsef', tgt, W1) + b1
        h = jax.nn.relu(h)
        o = jnp.einsum('bsef,edf->bsed', h, W2) + b2
        tgt2 = jnp.einsum('bsed,bse->bsd', o, router_w)
        return _layer_norm(tgt + tgt2, gamma, beta)
    x = L0_attn_x
    xn = _layernorm(x, axis=-1)
    x = x + _L0_attn_ref(xn, L0_attn_w_q, L0_attn_w_k, L0_attn_w_v, L0_attn_w_o) + _L0_ffn_ref(xn, L0_ffn_Wr, L0_ffn_br, L0_ffn_W1, L0_ffn_b1, L0_ffn_W2, L0_ffn_b2, L0_ffn_gamma, L0_ffn_beta)
    return x

_drawn_inputs = setup_inputs


def setup_inputs(seed=0):
    import zlib

    import numpy as np

    out = dict(_drawn_inputs(seed))
    spreads = {'L0_ffn_br': (0.0, 0.1),
     'L0_ffn_b1': (0.0, 0.1),
     'L0_ffn_b2': (0.0, 0.1),
     'L0_ffn_gamma': (1.0, 0.2),
     'L0_ffn_beta': (0.0, 0.1)}
    factors = {'L0_attn_w_q': 8.0, 'L0_attn_w_k': 8.0, 'L0_attn_w_v': 8.0, 'L0_attn_w_o': 8.0}
    for name, (base, spread) in spreads.items():
        noise = np.random.default_rng([zlib.crc32(name.encode()), seed]).standard_normal(out[name].shape)
        drawn = base * np.exp(spread * noise) if base else spread * noise
        out[name] = jnp.asarray(drawn.astype(out[name].dtype))
    for name, factor in factors.items():
        out[name] = (out[name] * factor).astype(out[name].dtype)
    return out
```

```python
import numpy as np

import concourse.bass as bass
from concourse import mybir
from contextlib import ExitStack

BATCH, SEQ, D = 16, 512, 128
HEADS, KV, HD = 16, 4, 8
REP = HEADS // KV
E, F = 8, 512
P = 128
T = SEQ // P
FC = F // P
QK = (HEADS + KV) * HD
QKV = QK + KV * HD
CAP, EPS, THETA = 50.0, 1e-5, 10000.0
TERMS = 8
ROWS = TERMS * HD
SLOT = 1024
MASKS = 7
SLOTS = 5


def diag_slots():
    place = {}
    for pair in range(2):
        first, second = (0, 1) if pair == 0 else (3, 4)
        for a in range(2):
            h = 2 * pair + a
            place[h, 0] = first * SLOT + 512 * a
            place[h, 1] = second * SLOT + 512 * a
            place[h, 3] = second * SLOT + 512 * a + 384
            place[h, 2] = 2 * SLOT + 512 * pair + 256 * a
    return place


PLACE = diag_slots()


def build_program(nc, x, w_q, w_k, w_v, w_o, b1t, w1t, w2t, wrt, br, b2, gamma, beta, rope, out):
    f32 = mybir.dt.float32
    bf16 = mybir.dt.bfloat16
    ALU = mybir.AluOpType
    ACT = mybir.ActivationFunctionType
    X = mybir.AxisListType.X
    ctx = ExitStack()
    with ctx:
        def sb(name, shape, dt=f32):
            return ctx.enter_context(nc.sbuf_tensor(name, shape, dt))

        def sem(name):
            return ctx.enter_context(nc.semaphore(name))

        x_res = sb("x_res", [P, BATCH * T * D])
        xn_all = sb("xn_all", [P, BATCH * T * D])
        w_qkv = sb("w_qkv", [P, QKV])
        w_out = sb("w_out", [P, D])
        cos2 = sb("cos2", [P, T, HEADS + KV, HD])
        sin2 = sb("sin2", [P, T, HEADS + KV, HD])
        ident = sb("ident", [P, P])
        ident_b = sb("ident_b", [P, P], bf16)
        minus_half = sb("minus_half", [P, T * (HEADS + KV)])
        xn = sb("xn", [P, T, D])
        xnT = sb("xnT", [P, T * P])
        stats = sb("stats", [P, T, 6])
        mv = sb("mv", [P, T, 2])
        var_eps = sb("var_eps", [P, T])
        rstd = sb("rstd", [P, T])
        qk = sb("qk", [P, T, HEADS + KV, HD])
        qk_a = sb("qk_a", [P, T, HEADS + KV, HD])
        qk_b = sb("qk_b", [P, T, HEADS + KV, HD])
        ms = sb("ms", [P, T * (HEADS + KV)])
        rms = sb("rms", [P, T * (HEADS + KV)])
        part1 = sb("part1", [P, T, HEADS + KV, HD], bf16)
        part2 = sb("part2", [P, T, HEADS + KV, HD], bf16)
        part3 = sb("part3", [P, T, HEADS + KV, HD], bf16)
        q_rows = sb("q_rows", [P, T, HEADS, TERMS, HD], bf16)
        k_rows = sb("k_rows", [P, T, KV, 2, TERMS, HD], bf16)
        qT = [sb(f"qT{i}", [P, HEADS // 2, SEQ], bf16) for i in range(2)]
        kT = [sb(f"kT{i}", [P, KV, 2, SEQ], bf16) for i in range(2)]
        v_aug = [sb(f"v_aug{i}", [P, T, KV, 32]) for i in range(2)]
        probs = [sb(f"probs{i}", [P, SLOTS * SLOT]) for i in range(2)]
        y_raw = [sb(f"y_raw{i}", [P, SEQ]) for i in range(2)]
        den = [sb(f"den{i}", [P, T * REP]) for i in range(2)]
        y_tok = sb("y_tok", [P, T, HEADS * HD])
        yT = sb("yT", [P, T * P])

        w1_sb = sb("w1_sb", [P, E * F])
        w2_sb = probs[1][:, 1024:5120].rearrange("p (k d) -> p k d", d=D)
        b1_sb = sb("b1_sb", [P, E * FC])
        b2_sb = probs[0][:, 0:E * D].rearrange("p (e d) -> p e d", e=E)
        gb = probs[0][:, 1024:1280].rearrange("p (e d) -> p e d", e=2)
        wr_sb = sb("wr_sb", [P, E])
        br_sb = sb("br_sb", [P, E])
        iota_e = sb("iota_e", [P, E])
        lg = sb("lg", [P, T, E])
        m8 = sb("m8", [P, T, 8])
        i8 = sb("i8", [P, T, 8], mybir.dt.uint32)
        i8f = sb("i8f", [P, T, 2])
        d21 = sb("d21", [P, T])
        e21 = sb("e21", [P, T])
        w12 = sb("w12", [P, T, 2])
        oh = sb("oh", [P, 2, T, E])
        rw = sb("rw", [P, T, E])
        zero1 = sb("zero1", [P, 1])
        ob = probs[0][:, 1536:2048].rearrange("p (t d) -> p t d", t=T)
        u = probs[0][:, 2048:2560].rearrange("p (t d) -> p t d", t=T)
        fin = [probs[0][:, 2560:3072].rearrange("p (t d) -> p t d", t=T)]
        hT = [probs[1][:, 0:512], probs[1][:, 512:1024]]

        ps_score = [ctx.enter_context(nc.psum_tensor(f"ps_score{i}", [P, SLOT], f32)) for i in range(2)]
        ps_y = ctx.enter_context(nc.psum_tensor("ps_y", [P, SEQ], f32))
        ps_misc = [ctx.enter_context(nc.psum_tensor(f"ps_misc{i}", [P, 512], f32)) for i in range(3)]

        ps_h = [ps_score[i // 2][:, 512 * (i % 2):512 * (i % 2) + 512] for i in range(4)]
        fw_loaded = sem("fw_loaded")
        g_loaded = sem("g_loaded")
        x_loaded = [sem(f"x_loaded{i}") for i in range(2)]
        w_loaded = sem("w_loaded")
        consts_made = sem("consts_made")
        var_ready, rstd_ready = sem("var_ready"), sem("rstd_ready")
        xn_ready = sem("xn_ready")
        misc_full, misc_free = sem("misc_full"), sem("misc_free")
        qk_ready, sq_ready = sem("qk_ready"), sem("sq_ready")
        ms_ready, rms_ready = sem("ms_ready"), sem("rms_ready")
        qkn_ready, rope_ready, rope_step = sem("qkn_ready"), sem("rope_ready"), sem("rope_step")
        rows_ready, split_ready = sem("rows_ready"), sem("split_ready")
        score_full, score_free = sem("score_full"), sem("score_free")
        exp_done, mask_done = sem("exp_done"), sem("mask_done")
        pv_done, y_free = sem("pv_done"), sem("y_free")
        den_ready, dve_stat = sem("den_ready"), sem("dve_stat")
        kT_half = sem("kT_half")
        dve_tick, pool_tick = sem("dve_tick"), sem("pool_tick")
        xn_copied = sem("xn_copied")
        attn_done = sem("attn_done")
        f_xn, f_xT_full, f_xT_free, f_lg_full = sem("f_xn"), sem("f_xT_full"), sem("f_xT_free"), sem("f_lg_full")
        f_h_full, f_h_free, f_relu = sem("f_h_full"), sem("f_h_free"), sem("f_relu")
        f_o_full, f_o_free, f_chain = sem("f_o_full"), sem("f_o_free"), sem("f_chain")
        f_exp, f_top = sem("f_exp"), sem("f_top")
        f_varr, f_rstd, f_out, f_stored = sem("f_varr"), sem("f_rstd"), sem("f_out"), [sem(f"f_stored{i}") for i in range(2)]

        PRE = 9
        BODY = 15
        LACK = 4

        def misc_index(b, k):
            if b is None:
                return k
            return PRE - LACK + BODY * b + k if not isinstance(b, int) or b > 0 else PRE + k

        def misc_bank(b, k):
            return (misc_index(None, k) if b is None else misc_index(0, k) if isinstance(b, int) and b == 0
                    else PRE - LACK + k) % 3

        class Misc:
            def __init__(self, eng, b):
                self.eng, self.b, self.k = eng, b, 0

            def fill(self):
                n = misc_index(self.b, self.k)
                bank = ps_misc[misc_bank(self.b, self.k)]
                if not isinstance(n, int) or n >= 3:
                    self.eng.wait_ge(misc_free, n - 2)
                self.k += 1
                return bank

            def drain(self):
                bank = ps_misc[misc_bank(self.b, self.k)]
                self.eng.wait_ge(misc_full, misc_index(self.b, self.k) + 1)
                self.k += 1
                return bank

        block = ctx.enter_context(nc.Block())

        def batches(eng, body):
            body(0, 0)
            with eng.Fori(0, BATCH // 2 - 1) as i:
                body(i * 2 + 1, 1)
                body(i * 2 + 2, 0)
            body(BATCH - 1, 1)

        def is_first(b):
            return isinstance(b, int) and b == 0

        def is_last(b):
            return isinstance(b, int) and b == BATCH - 1

        @block.sync
        def _(sp):
            def load(b, par):
                sp.dma_start(x_res[:, bass.ds(b * (T * D), T * D)].rearrange("p (t d) -> p t d", t=T),
                             x[bass.ds(b, 1), :, :].rearrange("o (t p) d -> p (o t) d", p=P)).then_inc(x_loaded[par], 16)
            for b in range(2):
                load(b, b)
            with sp.Fori(1, BATCH // 2) as i:
                b = i * 2
                for par in range(2):
                    sp.wait_ge(x_loaded[par], b * 8)
                    load(b + par, par)
            sp.wait_ge(x_loaded[0], 16 * (BATCH // 2))
            sp.wait_ge(x_loaded[1], 16 * (BATCH // 2))
            with sp.Fori(0, BATCH) as b:
                sp.wait_ge(f_out, b + 1)
                sp.dma_start(out[bass.ds(b, 1), :, :].rearrange("o (t p) d -> p (o t) d", p=P),
                             fin[0][:, :, :]).then_inc(f_stored[0], 16)
            sp.wait_ge(f_stored[0], 16 * BATCH)

        @block.gpsimd
        def _(pool):
            nc.gpsimd.memset(ident[:, :], 0.0).then_inc(consts_made, 1)
            nc.gpsimd.memset(minus_half[:, :], -0.5).then_inc(consts_made, 1)
            for i in range(2):
                nc.gpsimd.memset(v_aug[i][:, :, :, :], 0.0).then_inc(consts_made, 1)
                nc.gpsimd.memset(kT[i][:, :, :, :], 0.0).then_inc(consts_made, 1)
            pool.wait_ge(consts_made, 6)
            for i in range(2):
                nc.gpsimd.memset(v_aug[i][:, :, :, HD:HD + 1], 1.0).then_inc(consts_made, 1)
            nc.gpsimd.affine_select(out=ident[:, :], in_=ident[:, :], compare_op=ALU.not_equal, fill=1.0, base=0,
                                    pattern=[[-1, P]], channel_multiplier=1).then_inc(consts_made, 1)
            pool.wait_ge(consts_made, 9)
            nc.gpsimd.tensor_copy(ident_b[:, :], ident[:, :]).then_inc(consts_made, 1)
            pool.dma_start(w_qkv[:, 0:HEADS * HD], w_q).then_inc(w_loaded, 16)
            pool.dma_start(w_qkv[:, HEADS * HD:QK], w_k).then_inc(w_loaded, 16)
            pool.dma_start(w_qkv[:, QK:QKV], w_v).then_inc(w_loaded, 16)
            pool.dma_start(w_out[:, :], w_o).then_inc(w_loaded, 16)
            pool.dma_start(cos2[:, :, :, :], rope[0].rearrange("(t p) h d -> p t h d", p=P)).then_inc(w_loaded, 16)
            pool.dma_start(sin2[:, :, :, :], rope[1].rearrange("(t p) h d -> p t h d", p=P)).then_inc(w_loaded, 16)
            pool.wait_ge(w_loaded, 96)

            def ln_rstd(b):
                pool.wait_ge(var_ready, b + 1)
                nc.gpsimd.tensor_tensor(rstd[:, :], var_eps[:, :], minus_half[:, 0:T], ALU.pow).then_inc(rstd_ready, 1)

            def copy_xn(b):
                pool.wait_ge(xn_ready, b * 4 + 4)
                nc.gpsimd.tensor_copy(xn_all[:, bass.ds(b * (T * D), T * D)],
                                      xn[:, :, :].rearrange("p t d -> p (t d)")).then_inc(xn_copied, 1)

            def square(b):
                pool.wait_ge(qk_ready, 4 * b + 4)
                nc.gpsimd.tensor_tensor(qk_a[:, :, :, :], qk[:, :, :, :], qk[:, :, :, :], ALU.mult).then_inc(sq_ready, 1)

            def rms_factor(b):
                pool.wait_ge(ms_ready, 2 * b + 2)
                nc.gpsimd.tensor_tensor(rms[:, :], ms[:, :], minus_half[:, :], ALU.pow).then_inc(rms_ready, 1)

            def rotate(b):
                pool.wait_ge(qkn_ready, b + 1)
                nc.gpsimd.tensor_tensor(qk_a[:, :, :, :], qk[:, :, :, :], cos2[:, :, :, :], ALU.mult).then_inc(rope_step, 1)
                for half in range(2):
                    o = HD // 2 * half
                    s = HD // 2 * (1 - half)
                    nc.gpsimd.tensor_tensor(
                        qk_b[:, :, :, o:o + 4].rearrange("p t h d -> p (t h) d"),
                        qk[:, :, :, s:s + 4].rearrange("p t h d -> p (t h) d"),
                        sin2[:, :, :, o:o + 4].rearrange("p t h d -> p (t h) d"), ALU.mult).then_inc(rope_step, 1)
                pool.wait_ge(rope_step, 3 * b + 3)
                nc.gpsimd.tensor_tensor(qk_a[:, :, :, :], qk_a[:, :, :, :], qk_b[:, :, :, :], ALU.add).then_inc(rope_ready, 1)

            def mask(b, g, par, unit):
                n = b * 4 + g
                pool.wait_ge(exp_done, n * 2 + (unit + 1))
                pool.sem_inc(pool_tick, 1)
                buf = probs[g % 2]
                slots = (0, 1) if unit == 0 else (2, 3, 4)
                for s in slots:
                    v = buf[:, s * SLOT:(s + 1) * SLOT]
                    if s == 2:
                        parts = [v.rearrange("p (a c) -> p a c", c=2 * P)[:, :, 0:P]]
                    elif s in (0, 3):
                        parts = [v.rearrange("p (a c) -> p a c", c=4 * P)[:, :, 0:P]]
                    else:
                        parts = [v.rearrange("p (a c) -> p a c", c=4 * P)[:, :, i * P:(i + 1) * P] for i in (0, 3)]
                    for part in parts:
                        nc.gpsimd.affine_select(out=part, in_=part, compare_op=ALU.is_ge, fill=0.0, base=0,
                                                pattern=[[0, part.shape[1]], [1, P]], channel_multiplier=-1)\
                            .then_inc(mask_done, 1)

            ln_rstd(0)
            copy_xn(0)
            square(0)
            rms_factor(0)
            rotate(0)

            def body(b, par):
                last = is_last(b)
                if not last:
                    ln_rstd(b + 1)
                    copy_xn(b + 1)
                for g in range(KV):
                    if g == 1 and not last:
                        square(b + 1)
                        rms_factor(b + 1)
                    mask(b, g, par, 0)
                    if g == 1 and not last:
                        rotate(b + 1)
                    mask(b, g, par, 1)
            batches(pool, body)
            pool.wait_ge(pv_done, BATCH * KV)
            nc.gpsimd.iota(iota_e[:, :], pattern=[[1, E]], base=0, channel_multiplier=0, allow_small_or_imprecise_dtypes=True).then_inc(consts_made, 1)
            pool.wait_ge(consts_made, 11)
            pool.dma_start(w1_sb[:, :], w1t).then_inc(fw_loaded, 16)
            pool.dma_start(w2_sb[:, :, :], w2t).then_inc(fw_loaded, 16)
            pool.dma_start(b1_sb[:, :], b1t).then_inc(fw_loaded, 16)
            pool.dma_start(wr_sb[:, :], wrt).then_inc(fw_loaded, 16)
            pool.dma_start(br_sb[:, :], br.rearrange("(o e) -> o e", o=1).broadcast_to([P, E])).then_inc(fw_loaded, 16)
            pool.dma_start(b2_sb[:, :, :], b2.rearrange("(o e) d -> o e d", o=1).broadcast_to([P, E, D])).then_inc(fw_loaded, 16)
            pool.dma_start(gb[:, 0, :], gamma.rearrange("(o e) -> o e", o=1).broadcast_to([P, D])).then_inc(g_loaded, 16)
            pool.dma_start(gb[:, 1, :], beta.rearrange("(o e) -> o e", o=1).broadcast_to([P, D])).then_inc(g_loaded, 16)
            with pool.Fori(0, BATCH) as b:
                pool.wait_ge(f_varr, b + 1)
                nc.gpsimd.tensor_tensor(rstd[:, :], var_eps[:, :], minus_half[:, 0:T], ALU.pow).then_inc(f_rstd, 1)

        @block.scalar
        def _(act):
            def tanh(b, g, k):
                n = b * 4 + g
                act.wait_ge(score_full, n * SLOTS + (k + 1))
                if k == 0 and not (is_first(b) and g < 2):
                    act.wait_ge(pv_done, n - 1)
                nc.scalar.activation(probs[g % 2][:, k * SLOT:(k + 1) * SLOT], ps_score[(SLOTS * g + k) % 2][:, :],
                                     ACT.Tanh, scale=1.0 / (CAP * HD ** 0.5)).then_inc(score_free, 1)

            def exp(b, g, k0, k1):
                act.wait_ge(score_free, (b * 4 + g) * SLOTS + k1)
                v = probs[g % 2][:, k0 * SLOT:k1 * SLOT]
                nc.scalar.activation(v, v, ACT.Exp, scale=CAP).then_inc(exp_done, 1)

            def body(b, par):
                for g in range(KV):
                    tanh(b, g, 0)
                    tanh(b, g, 1)
                    exp(b, g, 0, 2)
                    tanh(b, g, 2)
                    tanh(b, g, 3)
                    tanh(b, g, 4)
                    exp(b, g, 2, SLOTS)
            batches(act, body)
            with act.Fori(0, BATCH) as b:
                act.wait_ge(f_top, b + 1)
                nc.scalar.activation(e21[:, :], d21[:, :], ACT.Exp).then_inc(f_exp, 1)
                for e in range(E):
                    for c in range(FC):
                        k = e * FC + c
                        act.wait_ge(f_h_full, b * (E * FC) + (k + 1))
                        if k >= 2:
                            act.wait_ge(f_h_free, b * (E * FC) + (k - 1))
                        nc.scalar.activation(hT[k % 2][:, :], ps_h[k % 4], ACT.Relu,
                                             bias=b1_sb[:, k:k + 1]).then_inc(f_relu, 1)

        @block.tensor
        def _(pe):
            pe.wait_ge(consts_made, 10)

            def scores(b, g, par, k):
                j = (b * 4 + g) * SLOTS + k
                if not (is_first(b) and SLOTS * g + k < 2):
                    pe.wait_ge(score_free, j - 1)
                dst = ps_score[(SLOTS * g + k) % 2]
                for (h, i), at in sorted(PLACE.items(), key=lambda it: it[1]):
                    if at // SLOT != k:
                        continue
                    head = REP * g + h
                    at -= k * SLOT
                    n = SEQ - P * i
                    last = nc.tensor.matmul(dst[:, at:at + n], kT[par][:, g, head % 2, i * P:(i + 1) * P],
                                            qT[par][:, head // 2, i * P:SEQ], start=(at % 512 == 0), stop=True,
                                            skip_group_check=True)
                last.then_inc(score_full, 1)

            def pv(b, g, par):
                n = b * 4 + g
                pe.wait_ge(mask_done, n * MASKS + MASKS)
                if not (is_first(b) and g == 0):
                    pe.wait_ge(y_free, n)
                for i in range(T):
                    for h in range(REP):
                        at = PLACE[h, i]
                        last = nc.tensor.matmul(ps_y[32 * h:32 * h + 32, i * P:SEQ], v_aug[par][:, i, g, :],
                                                probs[g % 2][:, at:at + SEQ - P * i], start=(i == 0), stop=(i == T - 1),
                                                skip_group_check=True)
                last.then_inc(pv_done, 1)

            def y_transpose(misc, b, g):
                pe.wait_ge(y_free, b * 4 + (g + 1))
                bank = misc.fill()
                for t in range(T):
                    last = nc.tensor.transpose(bank[:, t * P:(t + 1) * P], y_raw[g % 2][:, t * P:(t + 1) * P], ident[:, :])
                last.then_inc(misc_full, 1)

            def y_tok_transpose(misc, k_n):
                pe.wait_ge(misc_free, misc_index(*k_n) + 1)
                bank = misc.fill()
                for t in range(T):
                    last = nc.tensor.transpose(bank[:, t * P:(t + 1) * P], y_tok[:, t, :], ident[:, :])
                last.then_inc(misc_full, 1)

            def out_proj(misc, b, k_yT):
                pe.wait_ge(misc_free, misc_index(*k_yT) + 1)
                bank = misc.fill()
                for t in range(T):
                    last = nc.tensor.matmul(bank[:, t * P:(t + 1) * P], yT[:, t * P:(t + 1) * P], w_out[:, :],
                                            start=(t == 0), stop=True, skip_group_check=True)
                last.then_inc(misc_full, 1)

            def xn_transpose(misc, b):
                pe.wait_ge(xn_ready, b * 4 + 4)
                bank = misc.fill()
                for t in range(T):
                    last = nc.tensor.transpose(bank[:, t * P:(t + 1) * P], xn[:, t, :], ident[:, :])
                last.then_inc(misc_full, 1)

            def qkv(misc, k_xT):
                pe.wait_ge(misc_free, misc_index(*k_xT) + 1)
                for half in range(2):
                    bank = misc.fill()
                    for u in range(2):
                        t = 2 * half + u
                        last = nc.tensor.matmul(bank[:, u * QKV:(u + 1) * QKV], xnT[:, t * P:(t + 1) * P], w_qkv[:, :],
                                                start=(u == 0), stop=True, skip_group_check=True)
                    last.then_inc(misc_full, 1)

            def k_transpose(misc, b, which):
                pe.wait_ge(rows_ready, b * 9 + 9)
                bank = misc.fill()[:, :].bitcast(bf16)
                for u in range(2):
                    for t in range(T):
                        at = (u * T + t) * P
                        last = nc.tensor.transpose(bank[:, at:at + P],
                                                   k_rows[:, t, 2 * which + u, :, :, :].rearrange("p v r d -> p (v r d)"),
                                                   ident_b[:, :])
                last.then_inc(misc_full, 1)

            def q_transpose(misc, b, t):
                bank = misc.fill()[:, :].bitcast(bf16)
                for j in range(HEADS // 2):
                    last = nc.tensor.transpose(bank[:, j * P:(j + 1) * P],
                                               q_rows[:, t, 2 * j:2 * j + 2, :, :].rearrange("p h r d -> p (h r d)"),
                                               ident_b[:, :])
                last.then_inc(misc_full, 1)

            misc = Misc(pe, None)
            pe.wait_ge(w_loaded, 96)
            xn_transpose(misc, 0)
            qkv(misc, (None, 0))
            for which in range(2):
                k_transpose(misc, 0, which)
            for t in range(T):
                q_transpose(misc, 0, t)

            def body(b, par):
                misc = Misc(pe, b)
                first, last = is_first(b), is_last(b)
                for g in range(KV):
                    if g == 0:
                        pe.wait_ge(misc_free, misc_index(b, 0))
                    scores(b, g, par, 0)
                    scores(b, g, par, 1)
                    if g == 0:
                        if not first:
                            y_transpose(misc, b - 1, 2)
                        if not last:
                            k_x = (b, misc.k)
                            xn_transpose(misc, b + 1)
                    if g == 1 and not first:
                        k_n = (b, misc.k)
                        y_transpose(misc, b - 1, 3)
                    if g == 2:
                        if not first:
                            k_y = (b, misc.k)
                            y_tok_transpose(misc, k_n)
                        y_transpose(misc, b, 0)
                    if g == 3:
                        if not first:
                            out_proj(misc, b - 1, k_y)
                        y_transpose(misc, b, 1)
                        if not last:
                            for t in range(1, T):
                                q_transpose(misc, b + 1, t)
                    scores(b, g, par, 2)
                    scores(b, g, par, 3)
                    if g > 0:
                        pv(b, g - 1, par)
                    elif not first:
                        pv(b - 1, KV - 1, 1 - par)
                    scores(b, g, par, 4)
                    if not last:
                        if g == 0:
                            qkv(misc, k_x)
                        if g == 2:
                            k_transpose(misc, b + 1, 0)
                            k_transpose(misc, b + 1, 1)
                            q_transpose(misc, b + 1, 0)
                return misc
            batches(pe, body)
            b = BATCH - 1
            misc = Misc(pe, b)
            misc.k = BODY - PRE
            pv(b, KV - 1, 1)
            y_transpose(misc, b, 2)
            k_n = (b, misc.k)
            y_transpose(misc, b, 3)
            k_y = (b, misc.k)
            y_tok_transpose(misc, k_n)
            out_proj(misc, b, k_y)
            pe.wait_ge(attn_done, 1)
            pe.wait_ge(fw_loaded, 96)
            with pe.Fori(0, BATCH) as b:
                pe.wait_ge(f_xn, b + 1)
                for t in range(T):
                    last = nc.tensor.transpose(ps_misc[0][:, t * P:(t + 1) * P], xn[:, t, :], ident[:, :])
                last.then_inc(f_xT_full, 1)
                pe.wait_ge(f_xT_free, b + 1)
                for t in range(T):
                    last = nc.tensor.matmul(ps_misc[1][:, t * E:(t + 1) * E], xnT[:, t * P:(t + 1) * P], wr_sb[:, :],
                                            start=(t == 0), stop=True, skip_group_check=True)
                last.then_inc(f_lg_full, 1)
                def second(k):
                    e, c = k // FC, k % FC
                    pe.wait_ge(f_relu, b * (E * FC) + (k + 1))
                    if c == 0:
                        pe.wait_ge(f_o_free, b * E + (e + 1))
                    for t in range(T):
                        last = nc.tensor.matmul(ps_y[:, t * P:(t + 1) * P], hT[k % 2][:, t * P:(t + 1) * P],
                                                w2_sb[:, e * FC + c, :], start=(t == 0 and c == 0), stop=(c == FC - 1),
                                                skip_group_check=True)
                    last.then_inc(f_h_free, 1)
                for k in range(E * FC):
                    nc.tensor.matmul(ps_h[k % 4], w1_sb[:, k * P:(k + 1) * P], xnT[:, :], start=True, stop=True).then_inc(f_h_full, 1)
                    if k >= 1:
                        second(k - 1)
                second(E * FC - 1)

        @block.vector
        def _(dve):
            dve.wait_ge(consts_made, 10)

            def copy_out(bank, dst):
                return nc.vector.tensor_copy(dst, bank).then_inc(misc_free, 1)

            def layer_norm(b, par):
                dve.wait_ge(x_loaded[par], b * 8 + (16 if par == 0 else 8))
                for t in range(T):
                    nc.vector.bn_stats(stats[:, t, :], x_res[:, bass.ds(b * (T * D) + t * D, D)]).then_inc(dve_stat, 1)
                dve.wait_ge(dve_stat, b * 8 + 4)
                dve.sem_inc(dve_tick, 1)
                for t in range(T):
                    nc.vector.bn_aggr(mv[:, t, :], stats[:, t, :]).then_inc(dve_stat, 1)
                dve.wait_ge(dve_stat, b * 8 + 8)
                nc.vector.tensor_scalar(var_eps[:, :], mv[:, :, 1], EPS, None, ALU.add).then_inc(var_ready, 1)
                dve.wait_ge(rstd_ready, b + 1)
                if not is_first(b):
                    dve.wait_ge(xn_copied, b)
                for t in range(T):
                    nc.vector.tensor_scalar(xn[:, t, :], x_res[:, bass.ds(b * (T * D) + t * D, D)],
                                            mv[:, t, 0:1], rstd[:, t:t + 1], ALU.subtract, ALU.mult).then_inc(xn_ready, 1)

            def drain_xT(misc):
                copy_out(misc.drain()[:, :], xnT[:, :])

            def drain_qkv(misc, b, par):
                for half in range(2):
                    bank = misc.drain()[:, 0:2 * QKV].rearrange("p (u c) -> p u c", u=2)
                    nc.vector.tensor_copy(
                        qk[:, 2 * half:2 * half + 2, :, :].rearrange("p u h d -> p u (h d)"), bank[:, :, 0:QK]).then_inc(qk_ready, 1)
                    for u in range(2):
                        done = nc.vector.tensor_copy(
                            v_aug[par][:, 2 * half + u, :, 0:HD],
                            bank[:, u, QK:QKV].rearrange("p (g d) -> p g d", g=KV))
                        if u == 0:
                            done.then_inc(qk_ready, 1)
                    done.then_inc(misc_free, 1)

            def rms_norm(b):
                dve.wait_ge(sq_ready, b + 1)
                nc.vector.tensor_reduce(ms[:, :], qk_a[:, :, :, :].rearrange("p t h d -> p (t h) d"), X, ALU.add).then_inc(ms_ready, 1)
                dve.wait_ge(ms_ready, 2 * b + 1)
                nc.vector.tensor_scalar(ms[:, :], ms[:, :], 1.0 / HD, EPS, ALU.mult, ALU.add).then_inc(ms_ready, 1)

            def rms_scale(b):
                dve.wait_ge(rms_ready, b + 1)
                v = qk[:, :, :, :].rearrange("p t h d -> p (t h) d")
                nc.vector.tensor_tensor(v, v, rms[:, :].unsqueeze(2).broadcast_to([P, T * (HEADS + KV), HD]), ALU.mult).then_inc(qkn_ready, 1)

            def split(b):
                dve.wait_ge(rope_ready, b + 1)
                nc.vector.tensor_copy(part1[:, :, :, :], qk_a[:, :, :, :]).then_inc(split_ready, 1)
                dve.wait_ge(split_ready, 4 * b + 1)
                nc.vector.tensor_tensor(qk_b[:, :, :, :], qk_a[:, :, :, :], part1[:, :, :, :], ALU.subtract).then_inc(split_ready, 1)
                dve.wait_ge(split_ready, 4 * b + 2)
                nc.vector.tensor_copy(part2[:, :, :, :], qk_b[:, :, :, :]).then_inc(split_ready, 1)
                dve.wait_ge(split_ready, 4 * b + 3)
                nc.vector.tensor_tensor(part3[:, :, :, :], qk_b[:, :, :, :], part2[:, :, :, :], ALU.subtract).then_inc(split_ready, 1)
                dve.wait_ge(split_ready, 4 * b + 4)
                for n, part in enumerate((part1, part2, part3)):
                    c = len(range(n, TERMS, 3))
                    for var in range(2):
                        nc.vector.tensor_copy(
                            k_rows[:, :, :, var, n:TERMS:3, :],
                            part[:, :, HEADS:HEADS + KV, :].unsqueeze(3).broadcast_to([P, T, KV, c, HD])).then_inc(rows_ready, 1)
                    c = min(3, TERMS - 3 * n)
                    nc.vector.tensor_copy(
                        q_rows[:, :, :, 3 * n:3 * n + c, :],
                        part[:, :, 0:HEADS, :].unsqueeze(3).broadcast_to([P, T, HEADS, c, HD])).then_inc(rows_ready, 1)

            def drain_k(misc, par, which):
                bank = misc.drain()[:, :].bitcast(bf16).rearrange("p (u c) -> p u c", u=2)
                nc.vector.tensor_copy(kT[par][0:ROWS, 2 * which:2 * which + 2, 0, :], bank[0:ROWS]).then_inc(kT_half, 1)
                nc.vector.tensor_copy(kT[par][ROWS:P, 2 * which:2 * which + 2, 1, :], bank[ROWS:P]).then_inc(misc_free, 1)

            def drain_q(misc, par, t):
                bank = misc.drain()[:, :].bitcast(bf16).rearrange("p (j c) -> p j c", c=P)
                copy_out(bank, qT[par][:, :, t * P:(t + 1) * P])

            def take_y(b, g):
                dve.wait_ge(pv_done, b * 4 + (g + 1))
                nc.vector.tensor_copy(y_raw[g % 2][:, :], ps_y[:, :]).then_inc(y_free, 1)

            def normalise(misc, b, g):
                n = b * 4 + g
                bank = misc.drain()[:, :].rearrange("p (th c) -> p th c", c=32)
                nc.vector.reciprocal(den[g % 2][:, :], bank[:, :, HD]).then_inc(den_ready, 1)
                dve.wait_ge(den_ready, n + 1)
                nc.vector.tensor_tensor(
                    y_tok[:, :, g * REP * HD:(g + 1) * REP * HD].rearrange("p t (h d) -> p t h d", d=HD),
                    bank[:, :, 0:HD].rearrange("p (t h) d -> p t h d", t=T),
                    den[g % 2][:, :].rearrange("p (t h) -> p t h", t=T).unsqueeze(3).broadcast_to([P, T, REP, HD]),
                    ALU.mult).then_inc(misc_free, 1)

            def add_out(misc, b):
                bank = misc.drain()
                v = x_res[:, bass.ds(b * (T * D), T * D)]
                nc.vector.tensor_tensor(v, v, bank[:, :], ALU.add).then_inc(misc_free, 1)

            misc = Misc(dve, None)
            layer_norm(0, 0)
            drain_xT(misc)
            drain_qkv(misc, 0, 0)
            rms_norm(0)
            rms_scale(0)
            split(0)
            drain_k(misc, 0, 0)
            drain_k(misc, 0, 1)
            for t in range(T):
                drain_q(misc, 0, t)

            def body(b, par):
                misc = Misc(dve, b)
                first, last = is_first(b), is_last(b)
                if not first:
                    normalise(misc, b - 1, 2)
                if not last:
                    layer_norm(b + 1, 1 - par)
                    drain_xT(misc)
                if not first:
                    take_y(b - 1, 3)
                if not last:
                    drain_qkv(misc, b + 1, 1 - par)
                if not first:
                    normalise(misc, b - 1, 3)
                if not last:
                    rms_norm(b + 1)
                    rms_scale(b + 1)
                take_y(b, 0)
                if not last:
                    split(b + 1)
                if not first:
                    copy_out(misc.drain()[:, :], yT[:, :])
                normalise(misc, b, 0)
                take_y(b, 1)
                if not last:
                    drain_k(misc, 1 - par, 0)
                    drain_k(misc, 1 - par, 1)
                    drain_q(misc, 1 - par, 0)
                if not first:
                    add_out(misc, b - 1)
                normalise(misc, b, 1)
                if not last:
                    for t in range(1, T):
                        drain_q(misc, 1 - par, t)
                take_y(b, 2)
            batches(dve, body)
            b = BATCH - 1
            misc = Misc(dve, b)
            misc.k = BODY - PRE
            take_y(b, 3)
            normalise(misc, b, 2)
            normalise(misc, b, 3)
            copy_out(misc.drain()[:, :], yT[:, :])
            add_out(misc, b)
            dve.wait_ge(misc_free, BODY * BATCH)
            dve.wait_ge(fw_loaded, 96)
            dve.wait_ge(g_loaded, 32)
            nc.vector.memset(zero1[:, :], 0.0).then_inc(attn_done, 1)
            dve.wait_ge(attn_done, 1)
            nc.vector.memset(zero1[:, :], 0.0).then_inc(f_o_free, 1)
            chain = [0]
            with dve.Fori(0, BATCH) as b:
                chain[0] = 0
                N_CHAIN = 64

                def link(ins):
                    chain[0] += 1
                    ins.then_inc(f_chain, 1)
                    dve.wait_ge(f_chain, b * N_CHAIN + chain[0])
                    dve.sem_inc(dve_tick, 1)
                xb = xn_all[:, bass.ds(b * (T * D), T * D)]
                nc.vector.tensor_copy(xn[:, :, :].rearrange("p t d -> p (t d)"), xb).then_inc(f_xn, 1)
                dve.wait_ge(f_xT_full, b + 1)
                nc.vector.tensor_copy(xnT[:, :], ps_misc[0][:, :]).then_inc(f_xT_free, 1)
                dve.wait_ge(f_lg_full, b + 1)
                link(nc.vector.tensor_tensor(lg[:, :, :], ps_misc[1][:, 0:T * E].rearrange("p (t e) -> p t e", e=E),
                                             br_sb[:, :].unsqueeze(1).broadcast_to([P, T, E]), ALU.add))
                for t in range(T):
                    link(nc.vector.max(m8[:, t, :], lg[:, t, :]))
                for t in range(T):
                    link(nc.vector.max_index(i8[:, t, :], m8[:, t, :], lg[:, t, :]))
                link(nc.vector.tensor_copy(i8f[:, :, :], i8[:, :, 0:2]))
                nc.vector.tensor_tensor(d21[:, :], m8[:, :, 1], m8[:, :, 0], ALU.subtract).then_inc(f_top, 1)
                dve.wait_ge(f_exp, b + 1)
                link(nc.vector.tensor_scalar(w12[:, :, 0], e21[:, :], 1.0, None, ALU.add))
                link(nc.vector.reciprocal(w12[:, :, 0], w12[:, :, 0]))
                link(nc.vector.tensor_tensor(w12[:, :, 1], e21[:, :], w12[:, :, 0], ALU.mult))
                for j in range(2):
                    link(nc.vector.tensor_tensor(oh[:, j, :, :], iota_e[:, :].unsqueeze(1).broadcast_to([P, T, E]),
                                                 i8f[:, :, j:j + 1].broadcast_to([P, T, E]), ALU.is_equal))
                    link(nc.vector.tensor_tensor(oh[:, j, :, :], oh[:, j, :, :],
                                                 w12[:, :, j:j + 1].broadcast_to([P, T, E]), ALU.mult))
                link(nc.vector.tensor_tensor(rw[:, :, :], oh[:, 0, :, :], oh[:, 1, :, :], ALU.add))
                for e in range(E):
                    dve.wait_ge(f_h_free, b * (E * FC) + (e + 1) * FC)
                    nc.vector.tensor_tensor(ob[:, :, :], ps_y[:, :].rearrange("p (t d) -> p t d", t=T),
                                            b2_sb[:, e, :].unsqueeze(1).broadcast_to([P, T, D]), ALU.add).then_inc(f_o_free, 1)
                    dve.wait_ge(f_o_free, b * E + (e + 2))
                    for t in range(T):
                        ins = nc.vector.scalar_tensor_tensor(u[:, t, :], ob[:, t, :], rw[:, t, e:e + 1],
                                                             xn[:, t, :] if e == 0 else u[:, t, :], ALU.mult, ALU.add)
                        if t < T - 1:
                            ins.then_inc(f_chain, 1)
                            chain[0] += 1
                        else:
                            link(ins)
                for t in range(T):
                    link(nc.vector.bn_stats(stats[:, t, :], u[:, t, :]))
                for t in range(T):
                    link(nc.vector.bn_aggr(mv[:, t, :], stats[:, t, :]))
                nc.vector.tensor_scalar(var_eps[:, :], mv[:, :, 1], EPS, None, ALU.add).then_inc(f_varr, 1)
                dve.wait_ge(f_rstd, b + 1)
                for t in range(T):
                    link(nc.vector.tensor_scalar(u[:, t, :], u[:, t, :], mv[:, t, 0:1], rstd[:, t:t + 1], ALU.subtract, ALU.mult))
                link(nc.vector.tensor_tensor(u[:, :, :], u[:, :, :], gb[:, 0, :].unsqueeze(1).broadcast_to([P, T, D]), ALU.mult))
                link(nc.vector.tensor_tensor(u[:, :, :], u[:, :, :], gb[:, 1, :].unsqueeze(1).broadcast_to([P, T, D]), ALU.add))
                nc.vector.tensor_tensor(fin[0][:, :, :].rearrange("p t d -> p (t d)"), u[:, :, :].rearrange("p t d -> p (t d)"), x_res[:, bass.ds(b * (T * D), T * D)], ALU.add).then_inc(f_out, 1)
                assert chain[0] == N_CHAIN, chain[0]
                dve.wait_ge(f_stored[0], b * 16 + 16)


def kernel(**inputs):
    import concourse.bacc as bacc
    from concourse.bass_utils import run_bass_kernel_spmd

    nc = bacc.Bacc("TRN2", target_bir_lowering=False, num_devices=1)
    get = {n: np.asarray(a) for n, a in inputs.items()}
    inv_freq = (1.0 / THETA ** (np.arange(0, HD, 2, dtype=np.float32) / np.float32(HD))).astype(np.float32)
    angle = np.arange(SEQ, dtype=np.float32)[:, None] * inv_freq[None, :]
    cos, sin = np.cos(angle), np.sin(angle)
    rope = np.stack([np.concatenate([cos, cos], 1), np.concatenate([-sin, sin], 1)])
    rope = np.broadcast_to(rope[:, :, None, :], (2, SEQ, HEADS + KV, HD))
    laid = {
        "x": get["L0_attn_x"],
        "w_q": get["L0_attn_w_q"], "w_k": get["L0_attn_w_k"], "w_v": get["L0_attn_w_v"], "w_o": get["L0_attn_w_o"],
        "b1t": get["L0_ffn_b1"].reshape(E * FC, P).T,
        "w1t": get["L0_ffn_W1"].transpose(2, 0, 1).reshape(D, E * F),
        "w2t": get["L0_ffn_W2"].transpose(0, 2, 1).reshape(E * FC, P, D).transpose(1, 0, 2),
        "wrt": get["L0_ffn_Wr"].T,
        "br": get["L0_ffn_br"], "b2": get["L0_ffn_b2"], "gamma": get["L0_ffn_gamma"], "beta": get["L0_ffn_beta"],
        "rope": rope.astype(np.float32),
    }
    laid = {n: np.ascontiguousarray(a) for n, a in laid.items()}
    args = {n: nc.dram_tensor(f"in_{n}", a.shape, mybir.dt.from_np(a.dtype), kind="ExternalInput").ap() for n, a in laid.items()}
    out = nc.dram_tensor("out_0", (BATCH, SEQ, D), mybir.dt.float32, kind="ExternalOutput").ap()
    build_program(nc, out=out, **args)
    r = run_bass_kernel_spmd(nc, [{f"in_{n}": a for n, a in laid.items()}], core_ids=[0])
    return r.results[0]["out_0"]
```

```python
import numpy as np

import concourse.bass as bass
from concourse import mybir
from contextlib import ExitStack

BATCH, SEQ, D = 16, 512, 128
HEADS, KV, HD = 16, 4, 8
REP = HEADS // KV
E, F = 8, 512
P = 128
T = SEQ // P
FC = F // P
QK = (HEADS + KV) * HD
QKV = QK + KV * HD
CAP, EPS, THETA = 50.0, 1e-5, 10000.0
TERMS = 8
ROWS = TERMS * HD
SLOT = 1024
MASKS = 7
SLOTS = 5


TILES = BATCH * T
PICKS = 2
NT = TILES * PICKS + E - 1
LAG, H_LAG = 4, 2
FIRST_MOE, LAST_MOE = 4, 12
PER_BATCH = 18
NSLOT = (LAST_MOE - FIRST_MOE) * PER_BATCH
assert NSLOT >= NT + LAG
X_RING, O_RING = 9, 4
LEAD = X_RING // 2
W_RING, W_LEAD = 4, 1
T_RING = 3
E_TILES = LAG + NSLOT + W_LEAD
ZERO_ROWS = 10
SCATTERS = TILES * PICKS // (FIRST_MOE * KV)
NEWTON = 11


def diag_slots():
    place = {}
    for pair in range(2):
        first, second = (0, 1) if pair == 0 else (3, 4)
        for a in range(2):
            h = 2 * pair + a
            place[h, 0] = first * SLOT + 512 * a
            place[h, 1] = second * SLOT + 512 * a
            place[h, 3] = second * SLOT + 512 * a + 384
            place[h, 2] = 2 * SLOT + 512 * pair + 256 * a
    return place


PLACE = diag_slots()


def build_program(nc, x, w_q, w_k, w_v, w_o, b1t, w1t, w2t, wrt, br, b2, gamma, beta, rope, out):
    f32 = mybir.dt.float32
    bf16 = mybir.dt.bfloat16
    i32 = mybir.dt.int32
    ALU = mybir.AluOpType
    ACT = mybir.ActivationFunctionType
    X = mybir.AxisListType.X
    ctx = ExitStack()
    with ctx:
        def sb(name, shape, dt=f32):
            return ctx.enter_context(nc.sbuf_tensor(name, shape, dt))

        def sem(name):
            return ctx.enter_context(nc.semaphore(name))

        rows_in = nc.dram_tensor("rows_in", [-(-(NSLOT + LEAD) // ZERO_ROWS) * ZERO_ROWS * P, D], f32).ap()
        rows_out = nc.dram_tensor("rows_out", [NSLOT * P, D], f32).ap()

        x_res = sb("x_res", [P, BATCH * T * D])
        big = sb("big", [P, BATCH * T * D])
        xn_all = big
        w2_sb = big[:, 0:E * F]
        w_qkv = sb("w_qkv", [P, QKV])
        w_out = sb("w_out", [P, D])
        wr_sb = sb("wr_sb", [P, E])
        br_sb = sb("br_sb", [P, E])
        b1_sb = sb("b1_sb", [P, E * FC])
        b2_sb = sb("b2_sb", [P, E * D])
        gb = sb("gb", [P, 2, D])
        cos2 = sb("cos2", [P, T, HD])
        sin2 = sb("sin2", [P, T, HD])
        ident = sb("ident", [P, P])
        ident_b = sb("ident_b", [P, P], bf16)
        before = sb("before", [P, P], bf16)
        ones_b = sb("ones_b", [P, 1], bf16)
        rev_e = sb("rev_e", [P, E])
        slot_nr = sb("slot_nr", [1, E_TILES])
        mv = sb("mv", [P, TILES, 2])
        rstd = sb("rstd", [P, TILES])
        xn = sb("xn", [P, T, D])
        xnT = sb("xnT", [P, T * P])
        stats = [sb(f"stats{i}", [P, T, 6]) for i in range(2)]
        mv_tmp = [sb(f"mv_tmp{i}", [P, T, 2]) for i in range(2)]
        qk = sb("qk", [P, T, HEADS + KV, HD])
        qk_a = sb("qk_a", [P, T, HEADS + KV, HD])
        qk_b = sb("qk_b", [P, T, HEADS + KV, HD])
        ms = sb("ms", [P, T * (HEADS + KV)])
        rms = sb("rms", [P, T * (HEADS + KV)])
        rms_tmp = sb("rms_tmp", [P, T * (HEADS + KV)])
        parts = [sb(f"part{i}", [P, T, HEADS + KV, HD], bf16) for i in range(3)]
        q_rows = sb("q_rows", [P, T, HEADS, TERMS, HD], bf16)
        k_rows = sb("k_rows", [P, T, KV, 2, TERMS, HD], bf16)
        qT = [sb(f"qT{i}", [P, HEADS // 2, SEQ], bf16) for i in range(2)]
        kT = [sb(f"kT{i}", [P, KV, 2, SEQ], bf16) for i in range(2)]
        v_aug = [sb(f"v_aug{i}", [P, T, KV, 32]) for i in range(2)]
        probs = [sb(f"probs{i}", [P, SLOTS * SLOT]) for i in range(2)]
        y_raw = [sb(f"y_raw{i}", [P, SEQ]) for i in range(2)]
        den = [sb(f"den{i}", [P, T * REP]) for i in range(2)]
        y_tok = sb("y_tok", [P, T, HEADS * HD])
        yT = sb("yT", [P, T * P])
        pro_xn_buf = [xn[:, :, :], y_raw[1][:, :].rearrange("p (t d) -> p t d", t=T)]
        pro_xnT_buf = [xnT[:, :], yT[:, :]]
        weight = sb("weight", [P, PICKS, TILES])
        slot_i = sb("slot_i", [P, PICKS, TILES], i32)
        oslot_i = sb("oslot_i", [P, PICKS, TILES], i32)
        tile_e = sb("tile_e", [1, E_TILES], i32)

        space = sb("space", [P, 3968])

        def cuts(of=space):
            at = [0]

            def cut(n, dt=f32):
                v = of[:, at[0]:at[0] + n]
                at[0] += n
                assert at[0] <= of.shape[1], at[0]
                return v if dt == f32 else v.bitcast(dt)
            return cut

        cut = cuts()
        lg = cut(TILES * E).rearrange("p (t e) -> p t e", e=E)
        lg2 = cut(TILES * E).rearrange("p (t e) -> p t e", e=E)
        r_tmp = cut(TILES * E).rearrange("p (t e) -> p t e", e=E)
        oh = cut(PICKS * TILES * E).rearrange("p (j t e) -> p j t e", j=PICKS, e=E)
        oh_b = cut(PICKS * TILES * E // 2, bf16).rearrange("p (e c) -> p e c", e=E)
        m12 = cut(PICKS * TILES).rearrange("p (j t) -> p j t", j=PICKS)
        r_idx = cut(TILES)
        gap = cut(TILES)
        gap_e = cut(TILES)
        slot_f = cut(PICKS * TILES)
        nt, inc1, inc2, start = (cut(E) for _ in range(4))
        cnt_i = cut(E, i32)
        ve, nr_tmp = lg2.rearrange("p t e -> p (t e)")[:, 0:TILES], r_tmp.rearrange("p t e -> p (t e)")[:, 0:TILES]
        cut = cuts(probs[1])
        zero_rows = cut(ZERO_ROWS * D)
        cmp = cut((E - 1) * (E_TILES))[0:1].rearrange("p (e n) -> p e n", e=E - 1)
        tile_f = cut(E_TILES)[0:1]
        rank = cut(PICKS * TILES * E).rearrange("p (e c) -> p e c", e=E)
        tot_b = cut(E * P // 2, bf16).rearrange("p (e c) -> p e c", e=E)
        cut = cuts(big[:, E * F:])
        w1_t = [cut(F) for _ in range(W_RING)]
        xsT = [cut(P) for _ in range(T_RING)]
        hT = [cut(F) for _ in range(T_RING)]
        cut = cuts()
        o_row = [cut(D) for _ in range(O_RING)]
        xs = [cut(D) for _ in range(X_RING)]
        cut = cuts()
        picked = [cut(T * PICKS * D).rearrange("p (t j d) -> p t j d", t=T, j=PICKS) for _ in range(2)]
        u = cut(T * D).rearrange("p (t d) -> p t d", t=T)
        fin = [cut(T * D) for _ in range(2)]
        c_mv = cut(T * 2).rearrange("p (t k) -> p t k", t=T)
        c_ve, c_rstd, c_tmp = cut(T), cut(T), cut(T)

        ps_score = [ctx.enter_context(nc.psum_tensor(f"ps_score{i}", [P, SLOT], f32)) for i in range(2)]
        ps_y = ctx.enter_context(nc.psum_tensor("ps_y", [P, SEQ], f32))
        ps_misc = [ctx.enter_context(nc.psum_tensor(f"ps_misc{i}", [P, 512], f32)) for i in range(3)]

        x_loaded = [sem(f"x_loaded{i}") for i in range(2)]
        w_loaded, consts_made = sem("w_loaded"), sem("consts_made")
        zeroed, zero_made = sem("zeroed"), sem("zero_made")
        stat_done, mv_ready, ln_chain = sem("stat_done"), sem("mv_ready"), sem("ln_chain")
        pro_xn, pro_copied = sem("pro_xn"), sem("pro_copied")
        pro_xT_full, pro_xT_done = sem("pro_xT_full"), sem("pro_xT_done")
        pro_lg_full, pro_lg_done = sem("pro_lg_full"), sem("pro_lg_done")
        route, gap_ready, gap_exp, slots_ready = sem("route"), sem("gap_ready"), sem("gap_exp"), sem("slots_ready")
        onehot_ready = sem("onehot_ready")
        scattered = [sem(f"scattered{i}") for i in range(2)]
        tile_e_ready = sem("tile_e_ready")
        ew_loaded = sem("ew_loaded")
        xn_ready = sem("xn_ready")
        misc_full, misc_free = sem("misc_full"), sem("misc_free")
        qk_ready, sq_ready = sem("qk_ready"), sem("sq_ready")
        ms_ready, rms_chain = sem("ms_ready"), sem("rms_chain")
        qkn_ready, rope_ready, rope_step = sem("qkn_ready"), sem("rope_ready"), sem("rope_step")
        rows_ready, split_ready = sem("rows_ready"), sem("split_ready")
        kT_half = sem("kT_half")
        score_full, score_free = sem("score_full"), sem("score_free")
        exp_done, mask_done = sem("exp_done"), sem("mask_done")
        pv_done, y_free = sem("pv_done"), sem("y_free")
        den_ready = sem("den_ready")
        xs_loaded = [sem(f"xs_loaded{i}") for i in range(X_RING)]
        w1_loaded = [sem(f"w1_loaded{i}") for i in range(W_RING)]
        o_ready = sem("o_ready")
        o_stored = [sem(f"o_stored{i}") for i in range(O_RING)]
        space_clear = sem("space_clear")
        gathered = [sem(f"gathered{i}") for i in range(2)]
        c_chain, combined = sem("c_chain"), sem("combined")
        out_stored = [sem(f"out_stored{i}") for i in range(2)]
        dve_tick, pool_tick = sem("dve_tick"), sem("pool_tick")

        def order(first, last, moe, comb):
            def s(g, k):
                return ("scores", g, k)
            steps = (
                (s(0, 0), s(0, 1), "slot", ("y_transpose_prev", 2), "normalise_x", "x_transpose", "slot", s(0, 2), s(0, 3),
                 ("pv_prev", 3), "slot", s(0, 4), ("qkv", 0), ("qkv", 1), "slot"),
                (s(1, 0), s(1, 1), "slot", ("qk_rms", 0), ("y_transpose_prev", 3), "slot", s(1, 2), s(1, 3), ("qk_rms", 1),
                 "slot", ("pv", 0), "slot", s(1, 4), ("qk_rms", 2), "slot"),
                (s(2, 0), s(2, 1), "slot", "y_tok_transpose_prev", ("split", 0), "slot", ("y_transpose", 0), s(2, 2), s(2, 3),
                 ("pv", 1), "slot", ("split", 1), s(2, 4), "slot", "out_proj_prev", ("k_transpose", 0), ("k_transpose", 1),
                 ("q_transpose", 0), "slot"),
                (s(3, 0), s(3, 1), "slot", ("y_transpose", 1), ("q_transpose", 1), "slot", ("q_transpose", 2), s(3, 2), s(3, 3),
                 ("pv", 2), "slot", ("q_transpose", 3), s(3, 4), "slot"))
            out = []
            for g in range(KV):
                for part in steps[g]:
                    if part != "slot" or moe:
                        out.append(part if isinstance(part, tuple) else (part,))
                if comb:
                    out.append(("combine", g))
            if first:
                out = [o for o in out if not o[0].endswith("_prev")]
            if last:
                out = [o for o in out if o[0] not in ("normalise_x", "x_transpose", "qkv", "qk_rms", "split", "k_transpose", "q_transpose")]
            return out

        MISC = ("y_transpose_prev", "y_transpose", "y_tok_transpose_prev", "out_proj_prev", "x_transpose", "qkv",
                "k_transpose", "q_transpose")
        PRE = 9 + 4
        FIRST_USES, MID_USES = (sum(o[0] in MISC for o in order(k, False, False, False)) for k in (True, False))
        SLOT_USES = 2
        LAST_USES = sum(o[0] in MISC for o in order(False, True, False, False))
        MOE_USES = MID_USES + SLOT_USES * PER_BATCH
        assert MID_USES % 3 == 0 and sum(o[0] == "slot" for o in order(False, False, True, False)) == PER_BATCH

        def misc_base(b):
            if not isinstance(b, int):
                return b * MOE_USES - (MOE_USES * FIRST_MOE - misc_base(FIRST_MOE))
            if b == 0:
                return PRE
            return PRE + FIRST_USES + MID_USES * (b - 1) + SLOT_USES * PER_BATCH * (min(max(b, FIRST_MOE), LAST_MOE) - FIRST_MOE)

        class Misc:
            def __init__(self, eng, b):
                self.eng, self.k = eng, 0
                self.base = 0 if b is None else misc_base(b)
                self.phase = self.base % 3 if isinstance(self.base, int) else misc_base(FIRST_MOE) % 3

            def fill(self):
                n = self.base + self.k
                if not isinstance(n, int) or n >= 3:
                    self.eng.wait_ge(misc_free, n - 2)
                bank = ps_misc[(self.phase + self.k) % 3]
                self.k += 1
                return bank

            def drain(self):
                bank = ps_misc[(self.phase + self.k) % 3]
                self.k += 1
                self.eng.wait_ge(misc_full, self.base + self.k)
                return bank

        block = ctx.enter_context(nc.Block())

        def batches(body):
            for b in range(FIRST_MOE):
                body(b, b % 2)
            yield
            for b in range(LAST_MOE, BATCH):
                body(b, b % 2)
            yield

        def kind(b):
            number = isinstance(b, int)
            return number and b == 0, number and b == BATCH - 1, not number, number and b >= LAST_MOE

        def moe_batches(eng, body):
            with eng.Fori(FIRST_MOE // 2, LAST_MOE // 2) as i:
                body(i * 2, 0)
                body(i * 2 + 1, 1)

        def slot_number(b, s):
            return b * PER_BATCH - (FIRST_MOE * PER_BATCH - s) if FIRST_MOE * PER_BATCH >= s else b * PER_BATCH + (s - FIRST_MOE * PER_BATCH)

        def rounds(b, par, ring):
            per_batch = 16 * PER_BATCH // ring
            return (b - par) * per_batch - FIRST_MOE * per_batch

        @block.sync
        def _(sp):
            def load(b, par):
                sp.dma_start(x_res[:, bass.ds(b * (T * D), T * D)].rearrange("p (t d) -> p t d", t=T),
                             x[bass.ds(b, 1), :, :].rearrange("o (t p) d -> p (o t) d", p=P)).then_inc(x_loaded[par], 16)
            for b in range(2):
                load(b, b)
            with sp.Fori(1, BATCH // 2) as i:
                for par in range(2):
                    sp.wait_ge(x_loaded[par], i * 16)
                    load(i * 2 + par, par)
            sp.wait_ge(zero_made, 1)
            span = P * ZERO_ROWS
            for n in range(rows_in.shape[0] // span):
                sp.dma_start(rows_in[n * span:(n + 1) * span, :].rearrange("(p r) d -> p (r d)", r=ZERO_ROWS),
                             zero_rows).then_inc(zeroed, 16)
            sp.wait_ge(scattered[0], 16 * TILES)
            sp.dma_start(w2_sb.rearrange("p (k d) -> p k d", d=D), w2t).then_inc(ew_loaded, 16)
            sp.wait_ge(space_clear, 2)
            for k in range(O_RING):
                sp.dma_start(rows_out[k * P:(k + 1) * P, :], o_row[k]).then_inc(o_stored[k], 16)
            for k in range(O_RING):
                sp.wait_ge(o_stored[k], 16)

            def load_rows(n, k):
                sp.dma_start(xs[k % X_RING], rows_in[bass.ds(n * P, P), :]).then_inc(xs_loaded[k % X_RING], 16)

            def load_w1(n, k):
                e = sp.value_load(tile_e[0:1, bass.ds(n + LAG, 1)], min_val=0, max_val=E - 1)
                sp.dma_start(w1_t[k % W_RING], w1t[:, bass.ds(e * F, F)]).then_inc(w1_loaded[k % W_RING], 16)

            for n in range(LEAD):
                load_rows(n, n)
            for n in range(-H_LAG, W_LEAD):
                load_w1(n, n)
            with sp.Fori(0, NSLOT // (2 * PER_BATCH)) as i:
                for k in range(2 * PER_BATCH):
                    n = i * (2 * PER_BATCH) + k
                    load_rows(n + LEAD, k + LEAD)
                    sp.wait_ge(o_ready, n + 1)
                    load_w1(n + W_LEAD, k + W_LEAD)
                    sp.dma_start(rows_out[bass.ds(n * P, P), :], o_row[k % O_RING]).then_inc(o_stored[k % O_RING], 16)
            for c in range(BATCH):
                sp.wait_ge(combined, c + 1)
                sp.dma_start(out[c].rearrange("(t p) d -> p t d", p=P),
                             fin[c % 2].rearrange("p (t d) -> p t d", t=T)).then_inc(out_stored[c % 2], 16)
            for par in range(2):
                sp.wait_ge(out_stored[par], 16 * (BATCH // 2))

        @block.gpsimd
        def _(pool):
            nc.gpsimd.memset(ident[:, :], 0.0).then_inc(consts_made, 1)
            nc.gpsimd.memset(before[:, :], 1.0).then_inc(consts_made, 1)
            nc.gpsimd.memset(ones_b[:, :], 1.0).then_inc(consts_made, 1)
            for i in range(2):
                nc.gpsimd.memset(v_aug[i][:, :, :, :], 0.0).then_inc(consts_made, 1)
                nc.gpsimd.memset(kT[i][:, :, :, :], 0.0).then_inc(consts_made, 1)
            nc.gpsimd.iota(rev_e[:, :], pattern=[[-1, E]], base=E, channel_multiplier=0,
                           allow_small_or_imprecise_dtypes=True).then_inc(consts_made, 1)
            nc.gpsimd.iota(slot_nr[:, :], pattern=[[1, E_TILES]], base=-LAG, channel_multiplier=0,
                           allow_small_or_imprecise_dtypes=True).then_inc(consts_made, 1)
            pool.wait_ge(consts_made, 9)
            for i in range(2):
                nc.gpsimd.memset(v_aug[i][:, :, :, HD:HD + 1], 1.0).then_inc(consts_made, 1)
            nc.gpsimd.affine_select(out=ident[:, :], in_=ident[:, :], compare_op=ALU.not_equal, fill=1.0, base=0,
                                    pattern=[[-1, P]], channel_multiplier=1).then_inc(consts_made, 1)
            nc.gpsimd.affine_select(out=before[:, :], in_=before[:, :], compare_op=ALU.is_gt, fill=0.0, base=0,
                                    pattern=[[1, P]], channel_multiplier=-1).then_inc(consts_made, 1)
            pool.wait_ge(consts_made, 13)
            nc.gpsimd.tensor_copy(ident_b[:, :], ident[:, :]).then_inc(consts_made, 1)
            for dst, src in ((w_qkv[:, 0:HEADS * HD], w_q), (w_qkv[:, HEADS * HD:QK], w_k), (w_qkv[:, QK:QKV], w_v),
                             (w_out[:, :], w_o), (wr_sb[:, :], wrt), (b1_sb[:, :], b1t),
                             (cos2[:, :, :], rope[0].rearrange("(t p) d -> p t d", p=P)),
                             (sin2[:, :, :], rope[1].rearrange("(t p) d -> p t d", p=P)),
                             (br_sb[:, :], br.rearrange("(o e) -> o e", o=1).broadcast_to([P, E])),
                             (b2_sb[:, :], b2.rearrange("e d -> (e d)").rearrange("(o n) -> o n", o=1).broadcast_to([P, E * D])),
                             (gb[:, 0, :], gamma.rearrange("(o e) -> o e", o=1).broadcast_to([P, D])),
                             (gb[:, 1, :], beta.rearrange("(o e) -> o e", o=1).broadcast_to([P, D]))):
                pool.dma_start(dst, src).then_inc(w_loaded, 16)

            with pool.Fori(0, BATCH // 2) as i:
                for par in range(2):
                    b = i * 2 + par
                    pool.wait_ge(pro_xn, b * 4 + 4)
                    pool.sem_inc(pool_tick, 1)
                    nc.gpsimd.tensor_copy(xn_all[:, bass.ds(b * (T * D), T * D)],
                                          pro_xn_buf[par].rearrange("p t d -> p (t d)")).then_inc(pro_copied, 1)
            pool.wait_ge(w_loaded, 16 * 12)

            def mask(b, g, unit):
                pool.wait_ge(exp_done, (b * 4 + g) * 2 + (unit + 1))
                pool.sem_inc(pool_tick, 1)
                for s in (0, 1) if unit == 0 else (2, 3, 4):
                    v = probs[g % 2][:, s * SLOT:(s + 1) * SLOT]
                    if s == 2:
                        blocks = [v.rearrange("p (a c) -> p a c", c=2 * P)[:, :, 0:P]]
                    elif s in (0, 3):
                        blocks = [v.rearrange("p (a c) -> p a c", c=4 * P)[:, :, 0:P]]
                    else:
                        blocks = [v.rearrange("p (a c) -> p a c", c=4 * P)[:, :, i * P:(i + 1) * P] for i in (0, 3)]
                    for part in blocks:
                        nc.gpsimd.affine_select(out=part, in_=part, compare_op=ALU.is_ge, fill=0.0, base=0,
                                                pattern=[[0, part.shape[1]], [1, P]], channel_multiplier=-1)\
                            .then_inc(mask_done, 1)

            def scatter(n):
                t, j = n // PICKS, n % PICKS
                pool.indirect_dma_start(rows_in, bass.IndirectOffsetOnAxis(ap=slot_i[:, j, t:t + 1], axis=0),
                                        xn_all[:, t * D:(t + 1) * D], None).then_inc(scattered[t // (TILES // 2)], 16)

            def gather(c, t):
                for j in range(PICKS):
                    pool.indirect_dma_start(picked[c % 2][:, t, j, :], None, rows_out,
                                            bass.IndirectOffsetOnAxis(ap=oslot_i[:, j, c * T + t:c * T + t + 1], axis=0))\
                        .then_inc(gathered[c % 2], 16)

            def body(b, par):
                first, last, moe, comb = kind(b)
                for g in range(KV):
                    if first and g == 0:
                        pool.wait_ge(slots_ready, 1)
                        pool.wait_ge(zeroed, 16 * (rows_in.shape[0] // (P * ZERO_ROWS)))
                        pool.wait_ge(pro_copied, BATCH)
                    if comb:
                        c = (b - LAST_MOE) * KV + g
                        if c == 0:
                            for k in range(O_RING):
                                pool.wait_ge(o_stored[k], 16 * (NSLOT // O_RING + 1))
                        if c >= 2:
                            pool.wait_ge(combined, c - 1)
                    for unit in range(2):
                        mask(b, g, unit)
                        if not moe and not comb:
                            for n in range(SCATTERS // 2):
                                scatter((b * KV + g) * SCATTERS + unit * (SCATTERS // 2) + n)
                        if comb:
                            for t in range(T // 2):
                                gather(c, unit * (T // 2) + t)
            run = batches(body)
            next(run)
            moe_batches(pool, body)
            next(run)

        @block.scalar
        def _(act):
            def take_xT(b, par, first):
                act.wait_ge(pro_xT_full, b + 1)
                if not first:
                    act.wait_ge(pro_lg_full, b - 1)
                nc.scalar.activation(pro_xnT_buf[par], ps_score[par][:, 0:512], ACT.Copy).then_inc(pro_xT_done, 1)
            for b in range(2):
                take_xT(b, b, True)
            with act.Fori(1, BATCH // 2) as i:
                for par in range(2):
                    take_xT(i * 2 + par, par, False)

            def tanh(b, g, k):
                n = b * 4 + g
                act.wait_ge(score_full, n * SLOTS + (k + 1))
                if k == 0 and not (kind(b)[0] and g < 2):
                    act.wait_ge(pv_done, n - 1)
                nc.scalar.activation(probs[g % 2][:, k * SLOT:(k + 1) * SLOT], ps_score[(SLOTS * g + k) % 2][:, :],
                                     ACT.Tanh, scale=1.0 / (CAP * HD ** 0.5)).then_inc(score_free, 1)

            def exp(b, g, k0, k1):
                act.wait_ge(score_free, (b * 4 + g) * SLOTS + k1)
                v = probs[g % 2][:, k0 * SLOT:k1 * SLOT]
                nc.scalar.activation(v, v, ACT.Exp, scale=CAP).then_inc(exp_done, 1)

            def body(b, par):
                for g in range(KV):
                    if kind(b)[0] and g == 1:
                        act.wait_ge(zeroed, 16 * (rows_in.shape[0] // (P * ZERO_ROWS)))
                        act.wait_ge(gap_ready, 1)
                        nc.scalar.activation(gap_e, gap, ACT.Exp).then_inc(gap_exp, 1)
                        act.wait_ge(tile_e_ready, 1)
                    tanh(b, g, 0)
                    tanh(b, g, 1)
                    exp(b, g, 0, 2)
                    tanh(b, g, 2)
                    tanh(b, g, 3)
                    tanh(b, g, 4)
                    exp(b, g, 2, SLOTS)
            run = batches(body)
            next(run)
            moe_batches(act, body)
            next(run)

        @block.tensor
        def _(pe):
            pe.wait_ge(consts_made, 14)
            pe.wait_ge(w_loaded, 16 * 12)

            def pro_transpose(b, par, first):
                pe.wait_ge(pro_xn, b * 4 + 4)
                if not first:
                    pe.wait_ge(pro_xT_done, b - 1)
                for t in range(T):
                    last = nc.tensor.transpose(ps_score[par][:, t * P:(t + 1) * P], pro_xn_buf[par][:, t, :], ident[:, :])
                last.then_inc(pro_xT_full, 1)

            def logits(b, par):
                pe.wait_ge(pro_xT_done, b + 1)
                for t in range(T):
                    last = nc.tensor.matmul(ps_score[par][:, 512 + t * E:512 + (t + 1) * E], pro_xnT_buf[par][:, t * P:(t + 1) * P],
                                            wr_sb[:, :], start=(t == 0), stop=True, skip_group_check=True)
                last.then_inc(pro_lg_full, 1)

            pro_transpose(0, 0, True)
            pro_transpose(1, 1, True)
            logits(0, 0)
            with pe.Fori(1, BATCH // 2) as i:
                for par in range(2):
                    pro_transpose(i * 2 + par, par, False)
                    logits(i * 2 + par - 1, 1 - par)
            logits(BATCH - 1, 1)
            pe.wait_ge(pro_lg_done, BATCH)

            def scores(b, g, par, k):
                if not (kind(b)[0] and SLOTS * g + k < 2):
                    pe.wait_ge(score_free, (b * 4 + g) * SLOTS + (k - 1))
                dst = ps_score[(SLOTS * g + k) % 2]
                for (h, i), at in sorted(PLACE.items(), key=lambda it: it[1]):
                    if at // SLOT != k:
                        continue
                    head = REP * g + h
                    at -= k * SLOT
                    n = SEQ - P * i
                    last = nc.tensor.matmul(dst[:, at:at + n], kT[par][:, g, head % 2, i * P:(i + 1) * P],
                                            qT[par][:, head // 2, i * P:SEQ], start=(at % 512 == 0), stop=True,
                                            skip_group_check=True)
                last.then_inc(score_full, 1)

            def pv(b, g, par):
                n = b * 4 + g
                pe.wait_ge(mask_done, n * MASKS + MASKS)
                if not (kind(b)[0] and g == 0):
                    pe.wait_ge(y_free, n)
                for i in range(T):
                    for h in range(REP):
                        at = PLACE[h, i]
                        last = nc.tensor.matmul(ps_y[32 * h:32 * h + 32, i * P:SEQ], v_aug[par][:, i, g, :],
                                                probs[g % 2][:, at:at + SEQ - P * i], start=(i == 0), stop=(i == T - 1),
                                                skip_group_check=True)
                last.then_inc(pv_done, 1)

            def four_transposes(bank, part):
                for t in range(T):
                    last = nc.tensor.transpose(bank[:, t * P:(t + 1) * P], part(t), ident[:, :])
                last.then_inc(misc_full, 1)

            def y_transpose(misc, b, g):
                pe.wait_ge(y_free, b * 4 + (g + 1))
                four_transposes(misc.fill(), lambda t: y_raw[g % 2][:, t * P:(t + 1) * P])

            def y_tok_transpose(misc, used):
                pe.wait_ge(misc_free, used)
                four_transposes(misc.fill(), lambda t: y_tok[:, t, :])

            def out_proj(misc, used):
                pe.wait_ge(misc_free, used)
                bank = misc.fill()
                for t in range(T):
                    last = nc.tensor.matmul(bank[:, t * P:(t + 1) * P], yT[:, t * P:(t + 1) * P], w_out[:, :],
                                            start=(t == 0), stop=True, skip_group_check=True)
                last.then_inc(misc_full, 1)

            def x_transpose(misc, b):
                pe.wait_ge(xn_ready, b * 4 + 4)
                four_transposes(misc.fill(), lambda t: xn[:, t, :])

            def qkv(misc, half, used):
                pe.wait_ge(misc_free, used)
                bank = misc.fill()
                for v in range(2):
                    t = 2 * half + v
                    last = nc.tensor.matmul(bank[:, v * QKV:(v + 1) * QKV], xnT[:, t * P:(t + 1) * P], w_qkv[:, :],
                                            start=(v == 0), stop=True, skip_group_check=True)
                last.then_inc(misc_full, 1)

            def k_transpose(misc, b, which):
                pe.wait_ge(rows_ready, b * 9 + 9)
                bank = misc.fill()[:, :].bitcast(bf16)
                for v in range(2):
                    for t in range(T):
                        at = (v * T + t) * P
                        last = nc.tensor.transpose(bank[:, at:at + P],
                                                   k_rows[:, t, 2 * which + v, :, :, :].rearrange("p v r d -> p (v r d)"),
                                                   ident_b[:, :])
                last.then_inc(misc_full, 1)

            def q_transpose(misc, t):
                bank = misc.fill()[:, :].bitcast(bf16)
                for j in range(HEADS // 2):
                    last = nc.tensor.transpose(bank[:, j * P:(j + 1) * P],
                                               q_rows[:, t, 2 * j:2 * j + 2, :, :].rearrange("p h r d -> p (h r d)"),
                                               ident_b[:, :])
                last.then_inc(misc_full, 1)

            def expert_of(n, ahead):
                return pe.value_load(tile_e[0:1, bass.ds(n + ahead, 1)], min_val=0, max_val=E - 1)

            def slot(misc, b, par, s, before_it):
                n, k = slot_number(b, s), par * PER_BATCH + s
                e_out = expert_of(n, 0)
                bank = misc.fill()
                pe.wait_ge(xs_loaded[k % X_RING], rounds(b, par, X_RING) + 16 * (k // X_RING + 1))
                nc.tensor.transpose(bank[:, 0:P], xs[k % X_RING], ident[:, :])
                pe.wait_ge(misc_free, before_it)
                for c in range(FC):
                    last = nc.tensor.matmul(bank[:, P:2 * P], hT[(k - LAG) % T_RING][:, c * P:(c + 1) * P],
                                            w2_sb[:, bass.ds(e_out * F + c * P, P)], start=False, stop=(c == FC - 1),
                                            skip_group_check=True)
                last.then_inc(misc_full, 1)
                bank = misc.fill()
                m = k - H_LAG
                pe.wait_ge(w1_loaded[m % W_RING], rounds(b, par, W_RING) + 16 * (m // W_RING + 1 + (m % W_RING >= W_RING - H_LAG)))
                for c in range(FC):
                    last = nc.tensor.matmul(bank[:, c * P:(c + 1) * P], w1_t[m % W_RING][:, c * P:(c + 1) * P],
                                            xsT[m % T_RING], start=(c == 0), stop=True, skip_group_check=True)
                last.then_inc(misc_full, 1)

            misc = Misc(pe, None)
            x_transpose(misc, 0)
            for half in range(2):
                qkv(misc, half, 1)
            for which in range(2):
                k_transpose(misc, 0, which)
            for t in range(T):
                q_transpose(misc, t)

            pe.wait_ge(onehot_ready, PICKS)
            bank = misc.fill()
            for e in range(E):
                last = nc.tensor.matmul(bank[:, e:e + 1], oh_b[:, e, :], ones_b[:, :], start=(e == 0), stop=True,
                                        skip_group_check=True)
            last.then_inc(misc_full, 1)
            pe.wait_ge(misc_free, 10)
            bank = misc.fill()
            for e in range(E):
                last = nc.tensor.matmul(bank[:, e:e + 1], tot_b[:, e, :], ones_b[:, :], start=(e == 0), stop=True,
                                        skip_group_check=True)
            last.then_inc(misc_full, 1)
            half_e = E // 2
            for half in range(2):
                bank = misc.fill()
                nc.tensor.matmul(bank[:, :].rearrange("p (e c) -> p e c", e=half_e), before[:, :],
                                 oh_b[:, half * half_e:(half + 1) * half_e, :], start=True, stop=False, skip_group_check=True)
                for v in range(half_e):
                    last = nc.tensor.matmul(bank[:, v * P:(v + 1) * P], tot_b[:, half * half_e + v, :], before[:, :],
                                            start=False, stop=True, skip_group_check=True)
                last.then_inc(misc_full, 1)

            def body(b, par):
                misc = Misc(pe, b)
                first, last, moe, comb = kind(b)
                pe.wait_ge(misc_free, misc.base)
                s, ends = 0, [0, 0]
                for part, *a in order(first, last, moe, comb):
                    if part == "scores":
                        scores(b, a[0], par, a[1])
                    elif part == "pv":
                        pv(b, a[0], par)
                    elif part == "pv_prev":
                        pv(b - 1, a[0], 1 - par)
                    elif part in ("y_transpose", "y_transpose_prev"):
                        y_transpose(misc, b - (part != "y_transpose"), a[0])
                        if part == "y_transpose_prev":
                            y_used = misc.base + misc.k
                    elif part == "y_tok_transpose_prev":
                        y_tok_transpose(misc, y_used)
                        yT_used = misc.base + misc.k
                    elif part == "out_proj_prev":
                        out_proj(misc, yT_used)
                    elif part == "x_transpose":
                        x_transpose(misc, b + 1)
                        x_used = misc.base + misc.k
                    elif part == "qkv":
                        qkv(misc, a[0], x_used)
                    elif part == "k_transpose":
                        k_transpose(misc, b + 1, a[0])
                    elif part == "q_transpose":
                        q_transpose(misc, a[0])
                    elif part == "slot":
                        slot(misc, b, par, s, misc.base + ends[-2])
                        ends.append(misc.k)
                        s += 1
            run = batches(body)
            next(run)
            pe.wait_ge(ew_loaded, 16)
            pe.wait_ge(space_clear, 2)
            moe_batches(pe, body)
            next(run)
            b = BATCH - 1
            misc = Misc(pe, b)
            misc.k = LAST_USES
            pv(b, KV - 1, 1)
            y_transpose(misc, b, 2)
            y_transpose(misc, b, 3)
            y_tok_transpose(misc, misc.base + misc.k)
            out_proj(misc, misc.base + misc.k)

        @block.vector
        def _(dve):
            V = nc.vector

            V.memset(zero_rows, 0.0).then_inc(zero_made, 1)

            def newton(sem_, base, a, y, tmp):
                def link(ins, k):
                    ins.then_inc(sem_, 1)
                    if k < NEWTON:
                        dve.wait_ge(sem_, base + k)
                link(V.tensor_scalar(tmp.bitcast(i32), a.bitcast(i32), 1, None, ALU.logical_shift_right), 1)
                link(V.tensor_scalar(y.bitcast(i32), tmp.bitcast(i32), -1.0, float(0x5f3759df), ALU.mult, ALU.add), 2)
                for n in range(3):
                    link(V.tensor_tensor(tmp, y, y, ALU.mult), 3 * n + 3)
                    link(V.scalar_tensor_tensor(tmp, tmp, -0.5, a, ALU.mult, ALU.mult), 3 * n + 4)
                    link(V.scalar_tensor_tensor(y, tmp, 1.5, y, ALU.add, ALU.mult), 3 * n + 5)

            with dve.Fori(0, BATCH // 2) as i:
                for par in range(2):
                    b = i * 2 + par
                    dve.wait_ge(x_loaded[par], i * 16 + 16)
                    for t in range(T):
                        V.bn_stats(stats[par][:, t, :], x_res[:, bass.ds(b * (T * D) + t * D, D)]).then_inc(stat_done, 1)
                    dve.wait_ge(stat_done, b * 8 + 4)
                    dve.sem_inc(dve_tick, 1)
                    for t in range(T):
                        V.bn_aggr(mv_tmp[par][:, t, :], stats[par][:, t, :]).then_inc(stat_done, 1)
                    dve.wait_ge(stat_done, b * 8 + 8)
                    V.tensor_copy(mv[:, bass.ds(b * T, T), :], mv_tmp[par][:, :, :]).then_inc(mv_ready, 1)
            dve.wait_ge(mv_ready, BATCH)
            V.tensor_scalar(ve, mv[:, :, 1], EPS, None, ALU.add).then_inc(ln_chain, 1)
            dve.wait_ge(ln_chain, 1)
            newton(ln_chain, 1, ve, rstd[:, :], nr_tmp)
            dve.wait_ge(ln_chain, 1 + NEWTON)

            def normalise(b, dst, done):
                for t in range(T):
                    V.tensor_scalar(dst[:, t, :], x_res[:, bass.ds(b * (T * D) + t * D, D)],
                                    mv[:, bass.ds(b * T + t, 1), 0], rstd[:, bass.ds(b * T + t, 1)],
                                    ALU.subtract, ALU.mult).then_inc(done, 1)

            def take_logits(b, par):
                dve.wait_ge(pro_lg_full, b + 1)
                V.tensor_tensor(lg[:, bass.ds(b * T, T), :],
                                ps_score[par][:, 512:512 + T * E].rearrange("p (t e) -> p t e", e=E),
                                br_sb[:, :].unsqueeze(1).broadcast_to([P, T, E]), ALU.add).then_inc(pro_lg_done, 1)
            dve.wait_ge(w_loaded, 16 * 12)
            dve.wait_ge(consts_made, 14)
            normalise(0, pro_xn_buf[0], pro_xn)
            normalise(1, pro_xn_buf[1], pro_xn)
            take_logits(0, 0)
            with dve.Fori(1, BATCH // 2) as i:
                for par in range(2):
                    b = i * 2 + par
                    dve.wait_ge(pro_xT_full, b - 1)
                    dve.wait_ge(pro_copied, b - 1)
                    normalise(b, pro_xn_buf[par], pro_xn)
                    take_logits(b - 1, 1 - par)
            take_logits(BATCH - 1, 1)

            def take(misc, dst):
                bank = misc.drain()
                V.tensor_copy(dst, bank[:, :]).then_inc(misc_free, 1)

            def take_qkv(misc, par, half):
                bank = misc.drain()[:, 0:2 * QKV].rearrange("p (u c) -> p u c", u=2)
                V.tensor_copy(qk[:, 2 * half:2 * half + 2, :, :].rearrange("p u h d -> p u (h d)"),
                              bank[:, :, 0:QK]).then_inc(qk_ready, 1)
                V.tensor_copy(v_aug[par][:, 2 * half:2 * half + 2, :, 0:HD],
                              bank[:, :, QK:QKV].rearrange("p u (g d) -> p u g d", g=KV)).then_inc(misc_free, 1)

            def qk_square(b):
                dve.wait_ge(qk_ready, 2 * b + 2)
                V.tensor_tensor(qk_a[:, :, :, :], qk[:, :, :, :], qk[:, :, :, :], ALU.mult).then_inc(sq_ready, 1)
                dve.wait_ge(sq_ready, b + 1)
                V.tensor_reduce(ms[:, :], qk_a[:, :, :, :].rearrange("p t h d -> p (t h) d"), X, ALU.add).then_inc(ms_ready, 1)
                dve.wait_ge(ms_ready, 2 * b + 1)
                V.tensor_scalar(ms[:, :], ms[:, :], 1.0 / HD, EPS, ALU.mult, ALU.add).then_inc(ms_ready, 1)

            def qk_root(b):
                dve.wait_ge(ms_ready, 2 * b + 2)
                newton(rms_chain, b * NEWTON, ms[:, :], rms[:, :], rms_tmp[:, :])

            def qk_rotate(b):
                dve.wait_ge(rms_chain, b * NEWTON + NEWTON)
                v = qk[:, :, :, :].rearrange("p t h d -> p (t h) d")
                V.tensor_tensor(v, v, rms[:, :].unsqueeze(2).broadcast_to([P, T * (HEADS + KV), HD]), ALU.mult).then_inc(qkn_ready, 1)
                dve.wait_ge(qkn_ready, b + 1)
                V.tensor_tensor(qk_a[:, :, :, :], qk[:, :, :, :],
                                cos2[:, :, :].unsqueeze(2).broadcast_to([P, T, HEADS + KV, HD]), ALU.mult).then_inc(rope_step, 1)
                for half in range(2):
                    o, s = HD // 2 * half, HD // 2 * (1 - half)
                    V.tensor_tensor(
                        qk_b[:, :, :, o:o + HD // 2],
                        qk[:, :, :, s:s + HD // 2],
                        sin2[:, :, o:o + HD // 2].unsqueeze(2).broadcast_to([P, T, HEADS + KV, HD // 2]), ALU.mult).then_inc(rope_step, 1)
                dve.wait_ge(rope_step, 3 * b + 3)
                V.tensor_tensor(qk_a[:, :, :, :], qk_a[:, :, :, :], qk_b[:, :, :, :], ALU.add).then_inc(rope_ready, 1)

            def split(b):
                dve.wait_ge(rope_ready, b + 1)
                V.tensor_copy(parts[0][:, :, :, :], qk_a[:, :, :, :]).then_inc(split_ready, 1)
                dve.wait_ge(split_ready, 4 * b + 1)
                V.tensor_tensor(qk_b[:, :, :, :], qk_a[:, :, :, :], parts[0][:, :, :, :], ALU.subtract).then_inc(split_ready, 1)
                dve.wait_ge(split_ready, 4 * b + 2)
                V.tensor_copy(parts[1][:, :, :, :], qk_b[:, :, :, :]).then_inc(split_ready, 1)
                dve.wait_ge(split_ready, 4 * b + 3)
                V.tensor_tensor(parts[2][:, :, :, :], qk_b[:, :, :, :], parts[1][:, :, :, :], ALU.subtract).then_inc(split_ready, 1)

            def lay_rows(b):
                dve.wait_ge(split_ready, 4 * b + 4)
                for n, part in enumerate(parts):
                    c = len(range(n, TERMS, 3))
                    for var in range(2):
                        V.tensor_copy(k_rows[:, :, :, var, n:TERMS:3, :],
                                      part[:, :, HEADS:HEADS + KV, :].unsqueeze(3).broadcast_to([P, T, KV, c, HD])).then_inc(rows_ready, 1)
                    c = min(3, TERMS - 3 * n)
                    V.tensor_copy(q_rows[:, :, :, 3 * n:3 * n + c, :],
                                  part[:, :, 0:HEADS, :].unsqueeze(3).broadcast_to([P, T, HEADS, c, HD])).then_inc(rows_ready, 1)

            qk_rms = (qk_square, qk_root, qk_rotate)

            def take_k(misc, par, which):
                bank = misc.drain()[:, :].bitcast(bf16).rearrange("p (u c) -> p u c", u=2)
                V.tensor_copy(kT[par][0:ROWS, 2 * which:2 * which + 2, 0, :], bank[0:ROWS]).then_inc(kT_half, 1)
                V.tensor_copy(kT[par][ROWS:P, 2 * which:2 * which + 2, 1, :], bank[ROWS:P]).then_inc(misc_free, 1)

            def take_q(misc, par, t):
                bank = misc.drain()[:, :].bitcast(bf16).rearrange("p (j c) -> p j c", c=P)
                V.tensor_copy(qT[par][:, :, t * P:(t + 1) * P], bank).then_inc(misc_free, 1)

            def take_y(b, g):
                dve.wait_ge(pv_done, b * 4 + (g + 1))
                V.tensor_copy(y_raw[g % 2][:, :], ps_y[:, :]).then_inc(y_free, 1)

            def normalise_y(misc, b, g):
                bank = misc.drain()[:, :].rearrange("p (th c) -> p th c", c=32)
                V.reciprocal(den[g % 2][:, :], bank[:, :, HD]).then_inc(den_ready, 1)
                dve.wait_ge(den_ready, b * 4 + (g + 1))
                V.tensor_tensor(
                    y_tok[:, :, g * REP * HD:(g + 1) * REP * HD].rearrange("p t (h d) -> p t h d", d=HD),
                    bank[:, :, 0:HD].rearrange("p (t h) d -> p t h d", t=T),
                    den[g % 2][:, :].rearrange("p (t h) -> p t h", t=T).unsqueeze(3).broadcast_to([P, T, REP, HD]),
                    ALU.mult).then_inc(misc_free, 1)

            def add_out(misc, b):
                bank = misc.drain()
                v = x_res[:, bass.ds(b * (T * D), T * D)]
                V.tensor_tensor(v, v, bank[:, :], ALU.add).then_inc(misc_free, 1)

            def expert_of(n, ahead):
                return dve.value_load(tile_e[0:1, bass.ds(n + ahead, 1)], min_val=0, max_val=E - 1)

            def slot(misc, b, par, s):
                n, k = slot_number(b, s), par * PER_BATCH + s
                e_out, e_hid = expert_of(n, 0), expert_of(n, LAG - H_LAG)
                bank = misc.drain()
                V.tensor_copy(xsT[k % T_RING], bank[:, 0:P])
                dve.wait_ge(o_stored[k % O_RING], rounds(b, par, O_RING) + 16 * (k // O_RING + 1))
                V.tensor_tensor(o_row[k % O_RING], bank[:, P:2 * P], b2_sb[:, bass.ds(e_out * D, D)], ALU.add).then_inc(misc_free, 1)
                dve.wait_ge(misc_free, misc.base + misc.k)
                V.tensor_tensor(o_row[k % O_RING], o_row[k % O_RING], xs[(k - LAG) % X_RING], ALU.add).then_inc(o_ready, 1)
                bank = misc.drain()
                for c in range(FC):
                    last = V.tensor_scalar(hT[(k - H_LAG) % T_RING][:, c * P:(c + 1) * P], bank[:, c * P:(c + 1) * P],
                                           b1_sb[:, bass.ds(e_hid * FC + c, 1)], 0.0, ALU.add, ALU.max)
                last.then_inc(misc_free, 1)

            C_CHAIN = 5 * T + 3 + NEWTON

            def combine(c):
                base = c * C_CHAIN
                at = [0]

                def link(*many):
                    for ins in many:
                        ins.then_inc(c_chain, 1)
                    at[0] += len(many)
                    dve.wait_ge(c_chain, base + at[0])
                got = picked[c % 2]
                dve.wait_ge(gathered[c % 2], 16 * T * PICKS * (c // 2 + 1))
                w = [weight[:, j, :] for j in range(PICKS)]
                link(*[V.tensor_scalar(u[:, t, :], got[:, t, 0, :], w[0][:, c * T + t:c * T + t + 1], None, ALU.mult) for t in range(T)])
                link(*[V.scalar_tensor_tensor(u[:, t, :], got[:, t, 1, :], w[1][:, c * T + t:c * T + t + 1], u[:, t, :],
                                              ALU.mult, ALU.add) for t in range(T)])
                link(*[V.bn_stats(stats[0][:, t, :], u[:, t, :]) for t in range(T)])
                link(*[V.bn_aggr(c_mv[:, t, :], stats[0][:, t, :]) for t in range(T)])
                link(V.tensor_scalar(c_ve, c_mv[:, :, 1], EPS, None, ALU.add))
                newton(c_chain, base + at[0], c_ve, c_rstd, c_tmp)
                at[0] += NEWTON
                dve.wait_ge(c_chain, base + at[0])
                link(*[V.tensor_scalar(u[:, t, :], u[:, t, :], c_mv[:, t, 0:1], c_rstd[:, t:t + 1], ALU.subtract, ALU.mult) for t in range(T)])
                for k, op in ((0, ALU.mult), (1, ALU.add)):
                    link(V.tensor_tensor(u[:, :, :], u[:, :, :], gb[:, k, :].unsqueeze(1).broadcast_to([P, T, D]), op))
                if c >= 2:
                    dve.wait_ge(out_stored[c % 2], 16 * (c // 2))
                V.tensor_tensor(fin[c % 2], u.rearrange("p t d -> p (t d)"), x_res[:, c * T * D:(c + 1) * T * D],
                                ALU.add).then_inc(combined, 1)
                dve.wait_ge(combined, c + 1)
                assert at[0] == C_CHAIN, at[0]

            misc = Misc(dve, None)
            dve.wait_ge(pro_xT_full, BATCH)
            dve.wait_ge(pro_copied, BATCH)
            normalise(0, xn, xn_ready)
            take(misc, xnT[:, :])
            take_qkv(misc, 0, 0)
            take_qkv(misc, 0, 1)
            for stage in qk_rms:
                stage(0)
            split(0)
            lay_rows(0)
            take_k(misc, 0, 0)
            take_k(misc, 0, 1)
            for t in range(T):
                take_q(misc, 0, t)

            steps = [0]

            def link(ins):
                ins.then_inc(route, 1)
                steps[0] += 1
                dve.wait_ge(route, steps[0])
            dve.wait_ge(pro_lg_done, BATCH)
            by_e = [P, TILES, E]
            rev = rev_e[:, :].unsqueeze(1).broadcast_to(by_e)
            logits = lg
            for j in range(PICKS):
                link(V.tensor_reduce(m12[:, j, :], logits, X, ALU.max))
                link(V.tensor_tensor(r_tmp, logits, m12[:, j, :].unsqueeze(2).broadcast_to(by_e), ALU.is_equal))
                link(V.tensor_tensor(r_tmp, r_tmp, rev, ALU.mult))
                link(V.tensor_reduce(r_idx, r_tmp, X, ALU.max))
                link(V.tensor_tensor(oh[:, j, :, :], rev, r_idx.unsqueeze(2).broadcast_to(by_e), ALU.is_equal))
                V.tensor_copy(oh_b[:, :, j * TILES:(j + 1) * TILES], oh[:, j, :, :].rearrange("p t e -> p e t")).then_inc(onehot_ready, 1)
                if j == 0:
                    link(V.scalar_tensor_tensor(lg2.rearrange("p t e -> p (t e)"), oh[:, 0, :, :].rearrange("p t e -> p (t e)"),
                                                -1e30, lg.rearrange("p t e -> p (t e)"), ALU.mult, ALU.add))
                    logits = lg2
            V.tensor_tensor(gap, m12[:, 1, :], m12[:, 0, :], ALU.subtract).then_inc(gap_ready, 1)
            bank = misc.drain()
            V.tensor_copy(tot_b, bank[:, 0:E].unsqueeze(2).broadcast_to([P, E, P])).then_inc(misc_free, 1)
            bank = misc.drain()
            V.tensor_scalar(cnt_i, bank[:, 0:E], float(P - 1), None, ALU.add).then_inc(misc_free, 1)
            dve.wait_ge(misc_free, 11)
            link(V.tensor_scalar(cnt_i, cnt_i, 7, None, ALU.logical_shift_right))
            link(V.tensor_copy(nt, cnt_i))
            a, b_ = nt, inc1
            for sh in (1, 2, 4):
                link(V.tensor_copy(b_[:, 0:sh], a[:, 0:sh]))
                link(V.tensor_tensor(b_[:, sh:E], a[:, sh:E], a[:, 0:E - sh], ALU.add))
                a, b_ = b_, (inc2 if b_ is inc1 else inc1)
            incl = a
            link(V.tensor_tensor(start, incl, nt, ALU.subtract))
            link(V.tensor_scalar(start, start, float(P), None, ALU.mult))
            for half in range(2):
                bank = misc.drain()
                hv = slice(half * E // 2, (half + 1) * E // 2)
                V.tensor_tensor(rank[:, hv, :], bank[:, :].rearrange("p (e c) -> p e c", e=E // 2),
                                start[:, hv].unsqueeze(2).broadcast_to([P, E // 2, P]), ALU.add).then_inc(misc_free, 1)
            dve.wait_ge(misc_free, PRE)
            link(V.tensor_tensor(rank, rank, oh_b, ALU.mult))
            link(V.tensor_reduce(slot_f, rank.rearrange("p e c -> p c e"), X, ALU.add))
            V.tensor_copy(slot_i[:, :, :].rearrange("p j t -> p (j t)"), slot_f).then_inc(slots_ready, 1)
            link(V.tensor_scalar(oslot_i[:, :, :].rearrange("p j t -> p (j t)"), slot_f, float(LAG * P), None, ALU.add))
            n_all = E_TILES
            link(V.tensor_tensor(cmp, slot_nr[:, :].unsqueeze(1).broadcast_to([1, E - 1, n_all]),
                                 incl[0:1, 0:E - 1].unsqueeze(2).broadcast_to([1, E - 1, n_all]), ALU.is_ge))
            link(V.tensor_reduce(tile_f, cmp.rearrange("p e n -> p n e"), X, ALU.add))
            V.tensor_copy(tile_e[:, :], tile_f).then_inc(tile_e_ready, 1)

            def body(b, par):
                misc = Misc(dve, b)
                first, last, moe, comb = kind(b)
                s = 0
                for part, *a in order(first, last, moe, comb):
                    if part == "pv":
                        take_y(b, a[0])
                    elif part == "pv_prev":
                        take_y(b - 1, a[0])
                    elif part in ("y_transpose", "y_transpose_prev"):
                        normalise_y(misc, b - (part != "y_transpose"), a[0])
                    elif part == "y_tok_transpose_prev":
                        take(misc, yT[:, :])
                    elif part == "out_proj_prev":
                        add_out(misc, b - 1)
                    elif part == "normalise_x":
                        normalise(b + 1, xn, xn_ready)
                    elif part == "x_transpose":
                        take(misc, xnT[:, :])
                    elif part == "qkv":
                        take_qkv(misc, 1 - par, a[0])
                    elif part == "qk_rms":
                        qk_rms[a[0]](b + 1)
                    elif part == "split":
                        split(b + 1) if a[0] == 0 else lay_rows(b + 1)
                    elif part == "k_transpose":
                        take_k(misc, 1 - par, a[0])
                    elif part == "q_transpose":
                        take_q(misc, 1 - par, a[0])
                    elif part == "slot":
                        slot(misc, b, par, s)
                        s += 1
                    elif part == "combine":
                        c = (b - LAST_MOE) * KV + a[0] - 1
                        if c >= 0:
                            combine(c)
                    if first and part == "pv" and a[0] == 0:
                        dve.wait_ge(gap_exp, 1)
                        link(V.tensor_scalar(weight[:, 0, :], gap_e, 1.0, None, ALU.add))
                        link(V.reciprocal(weight[:, 0, :], weight[:, 0, :]))
                        link(V.tensor_tensor(weight[:, 1, :], gap_e, weight[:, 0, :], ALU.mult))
            run = batches(body)
            next(run)
            for half in range(2):
                dve.wait_ge(scattered[half], 16 * TILES)
            V.memset(big[:, E * F:], 0.0).then_inc(space_clear, 1)
            V.memset(space[:, :], 0.0).then_inc(space_clear, 1)
            dve.wait_ge(space_clear, 2)
            moe_batches(dve, body)
            next(run)
            b = BATCH - 1
            misc = Misc(dve, b)
            misc.k = LAST_USES
            take_y(b, 3)
            normalise_y(misc, b, 2)
            normalise_y(misc, b, 3)
            take(misc, yT[:, :])
            add_out(misc, b)
            dve.wait_ge(misc_free, misc.base + misc.k)
            combine(BATCH - 1)


def kernel(**inputs):
    import concourse.bacc as bacc
    from concourse.bass_utils import run_bass_kernel_spmd

    nc = bacc.Bacc("TRN2", target_bir_lowering=False, num_devices=1)
    get = {n: np.asarray(a) for n, a in inputs.items()}
    inv_freq = (1.0 / THETA ** (np.arange(0, HD, 2, dtype=np.float32) / np.float32(HD))).astype(np.float32)
    angle = np.arange(SEQ, dtype=np.float32)[:, None] * inv_freq[None, :]
    cos, sin = np.cos(angle), np.sin(angle)
    rope = np.stack([np.concatenate([cos, cos], 1), np.concatenate([-sin, sin], 1)])
    laid = {
        "x": get["L0_attn_x"],
        "w_q": get["L0_attn_w_q"], "w_k": get["L0_attn_w_k"], "w_v": get["L0_attn_w_v"], "w_o": get["L0_attn_w_o"],
        "b1t": get["L0_ffn_b1"].reshape(E * FC, P).T,
        "w1t": get["L0_ffn_W1"].transpose(2, 0, 1).reshape(D, E * F),
        "w2t": get["L0_ffn_W2"].transpose(0, 2, 1).reshape(E * FC, P, D).transpose(1, 0, 2),
        "wrt": get["L0_ffn_Wr"].T,
        "br": get["L0_ffn_br"], "b2": get["L0_ffn_b2"], "gamma": get["L0_ffn_gamma"], "beta": get["L0_ffn_beta"],
        "rope": rope.astype(np.float32),
    }
    laid = {n: np.ascontiguousarray(a) for n, a in laid.items()}
    args = {n: nc.dram_tensor(f"in_{n}", a.shape, mybir.dt.from_np(a.dtype), kind="ExternalInput").ap() for n, a in laid.items()}
    out = nc.dram_tensor("out_0", (BATCH, SEQ, D), mybir.dt.float32, kind="ExternalOutput").ap()
    build_program(nc, out=out, **args)
    r = run_bass_kernel_spmd(nc, [{f"in_{n}": a for n, a in laid.items()}], core_ids=[0])
    return r.results[0]["out_0"]
```

```python
import numpy as np

import concourse.bass as bass
from concourse import mybir
from contextlib import ExitStack

BATCH, SEQ, D = 16, 512, 128
HEADS, KV, HD = 16, 4, 8
REP = HEADS // KV
E, F = 8, 512
P = 128
T = SEQ // P
FC = F // P
QK = (HEADS + KV) * HD
QKV = QK + KV * HD
CAP, EPS, THETA = 50.0, 1e-5, 10000.0
TERMS = 8
ROWS = TERMS * HD
SLOT = 1024
MASKS = 7
SLOTS = 5


TILES = BATCH * T
PICKS = 2
NT = TILES * PICKS + E - 1
LAG, H_LAG = 4, 2
FIRST_MOE, LAST_MOE = 4, 12
PER_BATCH = 18
NSLOT = (LAST_MOE - FIRST_MOE) * PER_BATCH
assert NSLOT >= NT + LAG
X_RING, O_RING = 9, 4
LEAD = X_RING // 2
W_RING, W_LEAD = 4, 1
GROUPS = [range(0, 4), range(4, 8), range(8, 12), range(12, 14), range(14, 16)]
FINISH = {5: [0], 6: [1], 7: [2], 8: [3], 9: [4], 10: [5], 11: [6], 12: [7], 13: [8, 9], 14: [10, 11], 15: [12, 13]}
assert (BATCH - LAST_MOE) * KV == BATCH
X_LOADS = 4
MISC_RING = 2
HID_CREDIT = 2
T_RING = 3
E_TILES = LAG + NSLOT + W_LEAD
ZERO_ROWS = 10
SCATTERS = TILES * PICKS // (FIRST_MOE * KV)
NEWTON = 11


def diag_slots():
    place = {}
    for pair in range(2):
        first, second = (0, 1) if pair == 0 else (3, 4)
        for a in range(2):
            h = 2 * pair + a
            place[h, 0] = first * SLOT + 512 * a
            place[h, 1] = second * SLOT + 512 * a
            place[h, 3] = second * SLOT + 512 * a + 384
            place[h, 2] = 2 * SLOT + 512 * pair + 256 * a
    return place


PLACE = diag_slots()


def build_program(nc, x, w_q, w_k, w_v, w_o, b1t, w1t, w2t, wrt, br, b2, gamma, beta, rope, out):
    f32 = mybir.dt.float32
    bf16 = mybir.dt.bfloat16
    i32 = mybir.dt.int32
    ALU = mybir.AluOpType
    ACT = mybir.ActivationFunctionType
    X = mybir.AxisListType.X
    ctx = ExitStack()
    with ctx:
        def sb(name, shape, dt=f32):
            return ctx.enter_context(nc.sbuf_tensor(name, shape, dt))

        def sem(name):
            return ctx.enter_context(nc.semaphore(name))

        rows_in = nc.dram_tensor("rows_in", [-(-(NSLOT + LEAD) // ZERO_ROWS) * ZERO_ROWS * P, D], f32).ap()
        rows_out = nc.dram_tensor("rows_out", [NSLOT * P, D], f32).ap()

        x_res = sb("x_res", [P, BATCH * T * D])
        big = sb("big", [P, BATCH * T * D])
        xn_all = big
        w2_sb = big[:, 0:E * F]
        w_qkv = sb("w_qkv", [P, QKV])
        w_out = sb("w_out", [P, D])
        wr_sb = sb("wr_sb", [P, E])
        br_sb = sb("br_sb", [P, E])
        b1_sb = sb("b1_sb", [P, E * FC])
        b2_sb = sb("b2_sb", [P, E * D])
        gb = sb("gb", [P, 2, D])
        cos2 = sb("cos2", [P, T, HD])
        sin2 = sb("sin2", [P, T, HD])
        ident = sb("ident", [P, P])
        ident_b = sb("ident_b", [P, P], bf16)
        before = sb("before", [P, P], bf16)
        ones_b = sb("ones_b", [P, 1], bf16)
        rev_e = sb("rev_e", [P, E])
        slot_nr = sb("slot_nr", [1, E_TILES])
        mv = sb("mv", [P, TILES, 2])
        rstd = sb("rstd", [P, TILES])
        xn = sb("xn", [P, T, D])
        xnT = sb("xnT", [P, T * P])
        stats = [sb(f"stats{i}", [P, T, 6]) for i in range(2)]
        mv_tmp = [sb(f"mv_tmp{i}", [P, T, 2]) for i in range(2)]
        qk = sb("qk", [P, T, HEADS + KV, HD])
        qk_a = sb("qk_a", [P, T, HEADS + KV, HD])
        qk_b = sb("qk_b", [P, T, HEADS + KV, HD])
        ms = sb("ms", [P, T * (HEADS + KV)])
        rms = sb("rms", [P, T * (HEADS + KV)])
        rms_tmp = sb("rms_tmp", [P, T * (HEADS + KV)])
        parts = [sb(f"part{i}", [P, T, HEADS + KV, HD], bf16) for i in range(3)]
        q_rows = sb("q_rows", [P, T, HEADS, TERMS, HD], bf16)
        k_rows = sb("k_rows", [P, T, KV, 2, TERMS, HD], bf16)
        qT = [sb(f"qT{i}", [P, HEADS // 2, SEQ], bf16) for i in range(2)]
        kT = [sb(f"kT{i}", [P, KV, 2, SEQ], bf16) for i in range(2)]
        v_aug = [sb(f"v_aug{i}", [P, T, KV, 32]) for i in range(2)]
        probs = [sb(f"probs{i}", [P, SLOTS * SLOT]) for i in range(2)]
        y_raw = [sb(f"y_raw{i}", [P, SEQ]) for i in range(2)]
        den = [sb(f"den{i}", [P, T * REP]) for i in range(2)]
        y_tok = sb("y_tok", [P, T, HEADS * HD])
        yT = sb("yT", [P, T * P])
        pro_xn_buf = [xn[:, :, :], y_raw[1][:, :].rearrange("p (t d) -> p t d", t=T)]
        pro_xnT_buf = [xnT[:, :], yT[:, :]]
        weight = sb("weight", [P, PICKS, TILES])
        slot_i = sb("slot_i", [P, PICKS, TILES], i32)
        oslot_i = sb("oslot_i", [P, PICKS, TILES], i32)
        tile_e = sb("tile_e", [1, E_TILES], i32)

        space = sb("space", [P, 3968])

        def cuts(of=space):
            at = [0]

            def cut(n, dt=f32):
                v = of[:, at[0]:at[0] + n]
                at[0] += n
                assert at[0] <= of.shape[1], at[0]
                return v if dt == f32 else v.bitcast(dt)
            return cut

        cut = cuts()
        lg = cut(TILES * E).rearrange("p (t e) -> p t e", e=E)
        lg2 = cut(TILES * E).rearrange("p (t e) -> p t e", e=E)
        r_tmp = cut(TILES * E).rearrange("p (t e) -> p t e", e=E)
        oh = cut(PICKS * TILES * E).rearrange("p (j t e) -> p j t e", j=PICKS, e=E)
        oh_b = cut(PICKS * TILES * E // 2, bf16).rearrange("p (e c) -> p e c", e=E)
        m12 = cut(PICKS * TILES).rearrange("p (j t) -> p j t", j=PICKS)
        r_idx = cut(TILES)
        gap = cut(TILES)
        gap_e = cut(TILES)
        slot_f = cut(PICKS * TILES)
        nt, inc1, inc2, start = (cut(E) for _ in range(4))
        cnt_i = cut(E, i32)
        ve, nr_tmp = lg2.rearrange("p t e -> p (t e)")[:, 0:TILES], r_tmp.rearrange("p t e -> p (t e)")[:, 0:TILES]
        cut = cuts(probs[1])
        zero_rows = cut(ZERO_ROWS * D)
        cmp = cut((E - 1) * E_TILES)[0:1].rearrange("p (e n) -> p e n", e=E - 1)
        tile_f = cut(E_TILES)[0:1]
        rank = cut(PICKS * TILES * E).rearrange("p (e c) -> p e c", e=E)
        tot_b = cut(E * P // 2, bf16).rearrange("p (e c) -> p e c", e=E)
        cut = cuts(big[:, E * F:])
        w1_t = [cut(F) for _ in range(W_RING)]
        cut = cuts()
        xsT = [cut(P) for _ in range(T_RING)]
        hT = [cut(F) for _ in range(T_RING)]
        o_row = [cut(D) for _ in range(O_RING)]
        xs = [cut(D) for _ in range(X_RING)]
        cut = cuts()
        picked = [cut(T * PICKS * D).rearrange("p (t j d) -> p t j d", t=T, j=PICKS) for _ in range(2)]
        c_mv = cut(TILES * 2).rearrange("p (t k) -> p t k", k=2)
        c_ve, c_rstd, c_tmp, c_shift = (cut(TILES) for _ in range(4))
        u = big[:, :].rearrange("p (t d) -> p t d", d=D)

        ps_score = [ctx.enter_context(nc.psum_tensor(f"ps_score{i}", [P, SLOT], f32)) for i in range(2)]
        ps_y = ctx.enter_context(nc.psum_tensor("ps_y", [P, SEQ], f32))
        ps_hid = ctx.enter_context(nc.psum_tensor("ps_hid", [P, F], f32))
        ps_misc = [ctx.enter_context(nc.psum_tensor(f"ps_misc{i}", [P, 512], f32)) for i in range(MISC_RING)]

        x_loaded = [sem(f"x_loaded{i}") for i in range(X_LOADS)]
        w_loaded, consts_made = sem("w_loaded"), sem("consts_made")
        zeroed, zero_made = sem("zeroed"), sem("zero_made")
        stat_done, aggr_done, mv_ready, ln_chain = sem("stat_done"), sem("aggr_done"), sem("mv_ready"), sem("ln_chain")
        pro_xn, pro_copied = sem("pro_xn"), sem("pro_copied")
        pro_xT_full, pro_xT_done = sem("pro_xT_full"), sem("pro_xT_done")
        pro_lg_full, pro_lg_done = sem("pro_lg_full"), sem("pro_lg_done")
        route, gap_ready, gap_exp, slots_ready = sem("route"), sem("gap_ready"), sem("gap_exp"), sem("slots_ready")
        onehot_ready = sem("onehot_ready")
        scattered = [sem(f"scattered{i}") for i in range(2)]
        tile_e_ready = sem("tile_e_ready")
        ew_loaded = sem("ew_loaded")
        xn_ready = sem("xn_ready")
        misc_full, misc_free = sem("misc_full"), sem("misc_free")
        qk_ready, sq_ready = sem("qk_ready"), sem("sq_ready")
        ms_ready, rms_chain = sem("ms_ready"), sem("rms_chain")
        qkn_ready, rope_ready, rope_step = sem("qkn_ready"), sem("rope_ready"), sem("rope_step")
        rows_ready, split_ready = sem("rows_ready"), sem("split_ready")
        kT_half, kq_ready, beta_added = sem("kT_half"), sem("kq_ready"), sem("beta_added")
        score_full, score_free = sem("score_full"), sem("score_free")
        exp_done, mask_done = sem("exp_done"), sem("mask_done")
        pv_done, y_free = sem("pv_done"), sem("y_free")
        den_ready = sem("den_ready")
        xs_loaded = [sem(f"xs_loaded{i}") for i in range(X_RING)]
        w1_loaded = [sem(f"w1_loaded{i}") for i in range(W_RING)]
        hid_full, hid_free = sem("hid_full"), sem("hid_free")
        o_ready = sem("o_ready")
        o_stored = [sem(f"o_stored{i}") for i in range(O_RING)]
        space_clear = sem("space_clear")
        gathered = [sem(f"gathered{i}") for i in range(2)]
        scaled, summed, c_stats, c_mv_ready = sem("scaled"), sem("summed"), sem("c_stats"), sem("c_mv_ready")
        c_chain, c_rstd_ready, centred = sem("c_chain"), sem("c_rstd_ready"), sem("centred")
        fin_chain, combined = sem("fin_chain"), sem("combined")
        out_stored = sem("out_stored")
        dve_tick, pool_tick = sem("dve_tick"), sem("pool_tick")

        def order(first, last, moe, comb):
            def s(g, k):
                return ("scores", g, k)
            steps = (
                ("normalise_x", s(0, 0), s(0, 1), "slot", ("y_transpose_prev", 2), s(0, 2), "slot", ("exp", 0, 0), "x_transpose",
                 s(0, 3), "slot", ("pv_prev", 3, 0), s(0, 4), "slot", ("exp", 0, 1), ("pv_prev", 3, 1), ("qkv", 0), ("qkv", 1),
                 "slot"),
                (s(1, 0), s(1, 1), ("qk_rms", 0), "slot", ("y_transpose_prev", 3), s(1, 2), "slot", ("exp", 1, 0), s(1, 3),
                 ("qk_rms", 1), "slot", ("pv", 0, 0), s(1, 4), ("qk_rms", 2), "slot", ("exp", 1, 1), ("pv", 0, 1), ("qk_rms", 3)),
                (s(2, 0), s(2, 1), ("qk_rms", 4), "slot", "y_tok_transpose_prev", s(2, 2), ("split", 0), "slot", ("exp", 2, 0),
                 s(2, 3), ("split", 1), "slot", ("y_transpose", 0), ("pv", 1, 0), s(2, 4), ("split", 2), "slot", ("exp", 2, 1),
                 "out_proj_prev", ("pv", 1, 1), ("split", 3), "slot"),
                (s(3, 0), s(3, 1), ("k_transpose", 0), "slot", ("k_transpose", 1), s(3, 2), ("q_transpose", 0), "slot",
                 ("exp", 3, 0), ("y_transpose", 1), ("q_transpose", 1), s(3, 3), "slot", ("q_transpose", 2), ("q_transpose", 3),
                 ("pv", 2, 0), s(3, 4), "slot", ("exp", 3, 1), ("pv", 2, 1)))
            out = []
            for g, step in enumerate(steps):
                if not moe:
                    step = [part for part in step if part != "slot" and part[0] != "exp"]
                    step.insert(step.index(s(g, 1)) + 1, ("exp", g, 0))
                    step.insert(step.index(s(g, 4)) + 1, ("exp", g, 1))
                if comb:
                    step = [("centre", g)] + step + [("finish", g)]
                    step.insert(step.index(s(g, 2)), ("scale", g))
                    step.insert(step.index(s(g, 4)) + 1, ("sum", g))
                out += [part if isinstance(part, tuple) else (part,) for part in step]
            if first:
                out = [o for o in out if not o[0].endswith("_prev")]
            if last:
                out = [o for o in out if o[0] not in ("normalise_x", "x_transpose", "qkv", "qk_rms", "split", "k_transpose", "q_transpose")]
            return out

        MISC = ("y_transpose_prev", "y_transpose", "y_tok_transpose_prev", "out_proj_prev", "x_transpose", "qkv",
                "k_transpose", "q_transpose")
        PRE = 9 + 4
        FIRST_USES, MID_USES = (sum(o[0] in MISC for o in order(k, False, False, False)) for k in (True, False))
        SLOT_USES = 1
        LAST_USES = sum(o[0] in MISC for o in order(False, True, False, False))
        MOE_USES = MID_USES + SLOT_USES * PER_BATCH
        assert sum(o[0] == "slot" for o in order(False, False, True, False)) == PER_BATCH

        def misc_base(b):
            if not isinstance(b, int):
                return b * MOE_USES - (MOE_USES * FIRST_MOE - misc_base(FIRST_MOE))
            if b == 0:
                return PRE
            return PRE + FIRST_USES + MID_USES * (b - 1) + SLOT_USES * PER_BATCH * (min(max(b, FIRST_MOE), LAST_MOE) - FIRST_MOE)

        EARLY = [(0, k) for k in range(SLOTS)] + [(1, 0), (1, 1)]

        class Misc:
            def __init__(self, eng, b, par=0):
                self.eng, self.k = eng, 0
                self.base = 0 if b is None else misc_base(b)
                self.phase = self.base if isinstance(self.base, int) else misc_base(FIRST_MOE) + par * MOE_USES

            def fill(self):
                n = self.base + self.k
                if not isinstance(n, int) or n >= MISC_RING:
                    self.eng.wait_ge(misc_free, n - (MISC_RING - 1))
                bank = ps_misc[(self.phase + self.k) % MISC_RING]
                self.k += 1
                return bank

            def drain(self):
                bank = ps_misc[(self.phase + self.k) % MISC_RING]
                self.k += 1
                self.eng.wait_ge(misc_full, self.base + self.k)
                return bank

        block = ctx.enter_context(nc.Block())

        def batches(body):
            for b in range(FIRST_MOE):
                body(b, b % 2)
            yield
            for b in range(LAST_MOE, BATCH):
                body(b, b % 2)
            yield

        def kind(b):
            number = isinstance(b, int)
            return number and b == 0, number and b == BATCH - 1, not number, number and b >= LAST_MOE

        def moe_batches(eng, body):
            with eng.Fori(FIRST_MOE // 2, LAST_MOE // 2) as i:
                body(i * 2, 0)
                body(i * 2 + 1, 1)

        def slot_number(b, s):
            return b * PER_BATCH - (FIRST_MOE * PER_BATCH - s)

        def rounds(b, par, ring):
            per_batch = 16 * PER_BATCH // ring
            return (b - par) * per_batch - FIRST_MOE * per_batch

        @block.sync
        def _(sp):
            def load(b, q):
                sp.dma_start(x_res[:, bass.ds(b * (T * D), T * D)].rearrange("p (t d) -> p t d", t=T),
                             x[bass.ds(b, 1), :, :].rearrange("o (t p) d -> p (o t) d", p=P)).then_inc(x_loaded[q], 16)
            for q in range(X_LOADS):
                load(q, q)
            with sp.Fori(1, BATCH // X_LOADS) as i:
                for q in range(X_LOADS):
                    sp.wait_ge(x_loaded[q], i * 16)
                    load(i * X_LOADS + q, q)
            sp.wait_ge(zero_made, 1)
            span = P * ZERO_ROWS
            for n in range(rows_in.shape[0] // span):
                sp.dma_start(rows_in[n * span:(n + 1) * span, :].rearrange("(p r) d -> p (r d)", r=ZERO_ROWS),
                             zero_rows).then_inc(zeroed, 16)
            sp.wait_ge(scattered[0], 16 * TILES)
            sp.dma_start(w2_sb.rearrange("p (k d) -> p k d", d=D), w2t).then_inc(ew_loaded, 16)
            sp.wait_ge(space_clear, 1)
            for k in range(O_RING):
                sp.dma_start(rows_out[k * P:(k + 1) * P, :], o_row[k]).then_inc(o_stored[k], 16)
            for k in range(O_RING):
                sp.wait_ge(o_stored[k], 16)

            def load_rows(n, k):
                sp.dma_start(xs[k % X_RING], rows_in[bass.ds(n * P, P), :]).then_inc(xs_loaded[k % X_RING], 16)

            def load_w1(n, k):
                e = sp.value_load(tile_e[0:1, bass.ds(n + LAG, 1)], min_val=0, max_val=E - 1)
                sp.dma_start(w1_t[k % W_RING], w1t[:, bass.ds(e * F, F)]).then_inc(w1_loaded[k % W_RING], 16)

            sp.wait_ge(scattered[0], 16 * TILES)
            sp.wait_ge(scattered[1], 16 * TILES)
            for n in range(LEAD):
                load_rows(n, n)
            for n in range(-H_LAG, W_LEAD):
                load_w1(n, n)
            with sp.Fori(0, NSLOT // (2 * PER_BATCH)) as i:
                for k in range(2 * PER_BATCH):
                    n = i * (2 * PER_BATCH) + k
                    load_rows(n + LEAD, k + LEAD)
                    sp.wait_ge(o_ready, n + 1)
                    load_w1(n + W_LEAD, k + W_LEAD)
                    sp.dma_start(rows_out[bass.ds(n * P, P), :], o_row[k % O_RING]).then_inc(o_stored[k % O_RING], 16)
            for c in range(BATCH):
                sp.wait_ge(combined, c + 1)
                sp.dma_start(out[c].rearrange("(t p) d -> p t d", p=P), u[:, c * T:(c + 1) * T, :]).then_inc(out_stored, 16)
            sp.wait_ge(out_stored, 16 * BATCH)

        @block.gpsimd
        def _(pool):
            for dst, src in ((w_qkv[:, 0:HEADS * HD], w_q), (w_qkv[:, HEADS * HD:QK], w_k), (w_qkv[:, QK:QKV], w_v),
                             (w_out[:, :], w_o), (wr_sb[:, :], wrt), (b1_sb[:, :], b1t),
                             (cos2[:, :, :], rope[0].rearrange("(t p) d -> p t d", p=P)),
                             (sin2[:, :, :], rope[1].rearrange("(t p) d -> p t d", p=P)),
                             (br_sb[:, :], br.rearrange("(o e) -> o e", o=1).broadcast_to([P, E])),
                             (b2_sb[:, :], b2.rearrange("e d -> (e d)").rearrange("(o n) -> o n", o=1).broadcast_to([P, E * D])),
                             (gb[:, 0, :], gamma.rearrange("(o e) -> o e", o=1).broadcast_to([P, D])),
                             (gb[:, 1, :], beta.rearrange("(o e) -> o e", o=1).broadcast_to([P, D]))):
                pool.dma_start(dst, src).then_inc(w_loaded, 16)
            nc.gpsimd.memset(ident[:, :], 0.0).then_inc(consts_made, 1)
            nc.gpsimd.memset(before[:, :], 1.0).then_inc(consts_made, 1)
            nc.gpsimd.memset(ones_b[:, :], 1.0).then_inc(consts_made, 1)
            for i in range(2):
                nc.gpsimd.memset(v_aug[i][:, :, :, :], 0.0).then_inc(consts_made, 1)
                nc.gpsimd.memset(kT[i][:, :, :, :], 0.0).then_inc(consts_made, 1)
            nc.gpsimd.iota(rev_e[:, :], pattern=[[-1, E]], base=E, channel_multiplier=0,
                           allow_small_or_imprecise_dtypes=True).then_inc(consts_made, 1)
            nc.gpsimd.iota(slot_nr[:, :], pattern=[[1, E_TILES]], base=-LAG, channel_multiplier=0,
                           allow_small_or_imprecise_dtypes=True).then_inc(consts_made, 1)
            pool.wait_ge(consts_made, 9)
            for i in range(2):
                nc.gpsimd.memset(v_aug[i][:, :, :, HD:HD + 1], 1.0).then_inc(consts_made, 1)
            nc.gpsimd.affine_select(out=ident[:, :], in_=ident[:, :], compare_op=ALU.not_equal, fill=1.0, base=0,
                                    pattern=[[-1, P]], channel_multiplier=1).then_inc(consts_made, 1)
            nc.gpsimd.affine_select(out=before[:, :], in_=before[:, :], compare_op=ALU.is_gt, fill=0.0, base=0,
                                    pattern=[[1, P]], channel_multiplier=-1).then_inc(consts_made, 1)
            pool.wait_ge(consts_made, 13)
            nc.gpsimd.tensor_copy(ident_b[:, :], ident[:, :]).then_inc(consts_made, 1)
            with pool.Fori(0, BATCH // 2) as i:
                for par in range(2):
                    b = i * 2 + par
                    pool.wait_ge(pro_xn, b * 4 + 4)
                    pool.sem_inc(pool_tick, 1)
                    nc.gpsimd.tensor_copy(xn_all[:, bass.ds(b * (T * D), T * D)],
                                          pro_xn_buf[par].rearrange("p t d -> p (t d)")).then_inc(pro_copied, 1)
            pool.wait_ge(w_loaded, 16 * 12)

            def mask(b, g, unit):
                pool.wait_ge(exp_done, (b * 4 + g) * 2 + (unit + 1))
                pool.sem_inc(pool_tick, 1)
                for s in (0, 1) if unit == 0 else (2, 3, 4):
                    v = probs[g % 2][:, s * SLOT:(s + 1) * SLOT]
                    if s == 2:
                        blocks = [v.rearrange("p (a c) -> p a c", c=2 * P)[:, :, 0:P]]
                    elif s in (0, 3):
                        blocks = [v.rearrange("p (a c) -> p a c", c=4 * P)[:, :, 0:P]]
                    else:
                        blocks = [v.rearrange("p (a c) -> p a c", c=4 * P)[:, :, i * P:(i + 1) * P] for i in (0, 3)]
                    for part in blocks:
                        nc.gpsimd.affine_select(out=part, in_=part, compare_op=ALU.is_ge, fill=0.0, base=0,
                                                pattern=[[0, part.shape[1]], [1, P]], channel_multiplier=-1)\
                            .then_inc(mask_done, 1)

            def scatter(n):
                t, j = n // PICKS, n % PICKS
                pool.indirect_dma_start(rows_in, bass.IndirectOffsetOnAxis(ap=slot_i[:, j, t:t + 1], axis=0),
                                        xn_all[:, t * D:(t + 1) * D], None).then_inc(scattered[t // (TILES // 2)], 16)

            def gather(c, half):
                if half == 0 and c >= 2:
                    pool.wait_ge(summed, c - 1)
                for t in range(half * T // 2, (half + 1) * T // 2):
                    for j in range(PICKS):
                        pool.indirect_dma_start(picked[c % 2][:, t, j, :], None, rows_out,
                                                bass.IndirectOffsetOnAxis(ap=oslot_i[:, j, c * T + t:c * T + t + 1], axis=0))\
                            .then_inc(gathered[c % 2], 16)

            def body(b, par):
                first, last, moe, comb = kind(b)
                for g in range(KV):
                    if comb and b == LAST_MOE and g == 0:
                        for k in range(O_RING):
                            pool.wait_ge(o_stored[k], 16 * (NSLOT // O_RING + 1))
                        pool.wait_ge(misc_free, misc_base(LAST_MOE))
                        pool.wait_ge(hid_free, HID_CREDIT + NSLOT)
                        for k in range(X_RING):
                            pool.wait_ge(xs_loaded[k], 16 * len(range(k, NSLOT + LEAD, X_RING)))
                        for k in range(W_RING):
                            pool.wait_ge(w1_loaded[k], 16 * sum(m % W_RING == k for m in range(-H_LAG, NSLOT + W_LEAD)))
                        gather(0, 0)
                    for unit in range(2):
                        mask(b, g, unit)
                        if first and g == 0:
                            if unit == 0:
                                continue
                            pool.wait_ge(slots_ready, 1)
                            pool.wait_ge(zeroed, 16 * (rows_in.shape[0] // (P * ZERO_ROWS)))
                            pool.wait_ge(pro_copied, BATCH)
                            for n in range(SCATTERS):
                                scatter(n)
                        elif not moe and not comb:
                            for n in range(SCATTERS // 2):
                                scatter((b * KV + g) * SCATTERS + unit * (SCATTERS // 2) + n)
                        if comb:
                            half = 2 * ((b - LAST_MOE) * KV + g) + unit + 1
                            if half < 2 * BATCH:
                                gather(half // 2, half % 2)
            run = batches(body)
            next(run)
            moe_batches(pool, body)
            next(run)

        @block.scalar
        def _(act):
            def take_xT(b, par, first):
                act.wait_ge(pro_xT_full, b + 1)
                if not first:
                    act.wait_ge(pro_lg_full, b - 1)
                nc.scalar.activation(pro_xnT_buf[par], ps_score[par][:, 0:512], ACT.Copy).then_inc(pro_xT_done, 1)
            for b in range(2):
                take_xT(b, b, True)
            with act.Fori(1, BATCH // 2) as i:
                for par in range(2):
                    take_xT(i * 2 + par, par, False)

            def tanh(b, g, k):
                n = b * 4 + g
                act.wait_ge(score_full, n * SLOTS + (k + 1))
                if k == 0 and not (kind(b)[0] and g < 2):
                    act.wait_ge(pv_done, n - 1)
                nc.scalar.activation(probs[g % 2][:, k * SLOT:(k + 1) * SLOT], ps_score[(SLOTS * g + k) % 2][:, :],
                                     ACT.Tanh, scale=1.0 / (CAP * HD ** 0.5)).then_inc(score_free, 1)

            def hidden(b, par, s):
                n, k = slot_number(b, s), par * PER_BATCH + s
                e = act.value_load(tile_e[0:1, bass.ds(n + (LAG - H_LAG), 1)], min_val=0, max_val=E - 1)
                act.wait_ge(hid_full, n + 1)
                for c in range(FC):
                    last = nc.scalar.activation(hT[(k - H_LAG) % T_RING][:, c * P:(c + 1) * P], ps_hid[:, c * P:(c + 1) * P],
                                                ACT.Relu, bias=b1_sb[:, bass.ds(e * FC + c, 1)])
                last.then_inc(hid_free, 1)

            def scale(c):
                act.wait_ge(gathered[c % 2], 16 * T * PICKS * (c // 2 + 1))
                for t in range(T):
                    v = picked[c % 2][:, t, 1, :]
                    last = nc.scalar.activation(v, v, ACT.Copy, scale=weight[:, 1, c * T + t:c * T + t + 1])
                last.then_inc(scaled, 1)

            def centre(c):
                act.wait_ge(c_rstd_ready, 1 + [c in group for group in GROUPS].index(True))
                for t in range(c * T, (c + 1) * T):
                    last = nc.scalar.activation(u[:, t, :], u[:, t, :], ACT.Identity, scale=c_rstd[:, t:t + 1], bias=c_shift[:, t:t + 1])
                last.then_inc(centred, 1)

            def exp(b, g, k0, k1):
                act.wait_ge(score_free, (b * 4 + g) * SLOTS + k1)
                v = probs[g % 2][:, k0 * SLOT:k1 * SLOT]
                nc.scalar.activation(v, v, ACT.Exp, scale=CAP).then_inc(exp_done, 1)

            def body(b, par):
                s = 0
                for part, *a in order(*kind(b)):
                    if part == "slot":
                        hidden(b, par, s)
                        s += 1
                    elif part == "exp":
                        exp(b, a[0], *((0, 2) if a[1] == 0 else (2, SLOTS)))
                    elif part == "centre":
                        for c in FINISH.get((b - LAST_MOE) * KV + a[0], ()):
                            centre(c)
                    elif part == "scale":
                        if (b - LAST_MOE) * KV + a[0] >= 1:
                            scale((b - LAST_MOE) * KV + a[0] - 1)
                    elif part == "scores":
                        if kind(b)[0] and a == [1, 0]:
                            act.wait_ge(zeroed, 16 * (rows_in.shape[0] // (P * ZERO_ROWS)))
                            act.wait_ge(gap_ready, 1)
                            nc.scalar.activation(gap_e, gap, ACT.Exp).then_inc(gap_exp, 1)
                            act.wait_ge(tile_e_ready, 1)
                        tanh(b, *a)
            run = batches(body)
            next(run)
            act.sem_inc(hid_free, HID_CREDIT)
            moe_batches(act, body)
            next(run)
            scale(BATCH - 1)
            for c in GROUPS[-1]:
                centre(c)

        @block.tensor
        def _(pe):
            pe.wait_ge(consts_made, 14)
            pe.wait_ge(w_loaded, 16 * 12)

            def pro_transpose(b, par, first):
                pe.wait_ge(pro_xn, b * 4 + 4)
                if not first:
                    pe.wait_ge(pro_xT_done, b - 1)
                for t in range(T):
                    last = nc.tensor.transpose(ps_score[par][:, t * P:(t + 1) * P], pro_xn_buf[par][:, t, :], ident[:, :])
                last.then_inc(pro_xT_full, 1)

            def logits(b, par, first):
                if not first:
                    pe.wait_ge(pro_lg_done, b - 1)
                pe.wait_ge(pro_xT_done, b + 1)
                for t in range(T):
                    last = nc.tensor.matmul(ps_score[par][:, 512 + t * E:512 + (t + 1) * E], pro_xnT_buf[par][:, t * P:(t + 1) * P],
                                            wr_sb[:, :], start=(t == 0), stop=True, skip_group_check=True)
                last.then_inc(pro_lg_full, 1)

            pro_transpose(0, 0, True)
            pro_transpose(1, 1, True)
            logits(0, 0, True)
            pro_transpose(2, 0, False)
            logits(1, 1, True)
            pro_transpose(3, 1, False)
            with pe.Fori(2, BATCH // 2) as i:
                for par in range(2):
                    logits(i * 2 + par - 2, par, False)
                    pro_transpose(i * 2 + par, par, False)
            logits(BATCH - 2, 0, False)
            logits(BATCH - 1, 1, False)
            pe.wait_ge(pro_lg_done, BATCH)

            def scores(b, g, par, k):
                if not (kind(b)[0] and SLOTS * g + k < 2):
                    pe.wait_ge(score_free, (b * 4 + g) * SLOTS + (k - 1))
                dst = ps_score[(SLOTS * g + k) % 2]
                for (h, i), at in sorted(PLACE.items(), key=lambda it: it[1]):
                    if at // SLOT != k:
                        continue
                    head = REP * g + h
                    at -= k * SLOT
                    n = SEQ - P * i
                    last = nc.tensor.matmul(dst[:, at:at + n], kT[par][:, g, head % 2, i * P:(i + 1) * P],
                                            qT[par][:, head // 2, i * P:SEQ], start=(at % 512 == 0), stop=True,
                                            skip_group_check=True)
                last.then_inc(score_full, 1)

            def pv(b, g, par, half):
                n = b * 4 + g
                if half == 0:
                    pe.wait_ge(mask_done, n * MASKS + MASKS)
                    if not (kind(b)[0] and g == 0):
                        pe.wait_ge(y_free, n)
                for i in (0,) if half == 0 else range(1, T):
                    for h in range(REP):
                        at = PLACE[h, i]
                        last = nc.tensor.matmul(ps_y[32 * h:32 * h + 32, i * P:SEQ], v_aug[par][:, i, g, :],
                                                probs[g % 2][:, at:at + SEQ - P * i], start=(i == 0), stop=(i == T - 1),
                                                skip_group_check=True)
                if half == 1:
                    last.then_inc(pv_done, 1)

            def four_transposes(bank, part):
                for t in range(T):
                    last = nc.tensor.transpose(bank[:, t * P:(t + 1) * P], part(t), ident[:, :])
                last.then_inc(misc_full, 1)

            def y_transpose(misc, b, g):
                pe.wait_ge(y_free, b * 4 + (g + 1))
                four_transposes(misc.fill(), lambda t: y_raw[g % 2][:, t * P:(t + 1) * P])

            def y_tok_transpose(misc, used):
                pe.wait_ge(misc_free, used)
                four_transposes(misc.fill(), lambda t: y_tok[:, t, :])

            def out_proj(misc, used):
                pe.wait_ge(misc_free, used)
                bank = misc.fill()
                for t in range(T):
                    last = nc.tensor.matmul(bank[:, t * P:(t + 1) * P], yT[:, t * P:(t + 1) * P], w_out[:, :],
                                            start=(t == 0), stop=True, skip_group_check=True)
                last.then_inc(misc_full, 1)

            def x_transpose(misc, b):
                pe.wait_ge(xn_ready, b * 4 + 4)
                four_transposes(misc.fill(), lambda t: xn[:, t, :])

            def qkv(misc, half, used):
                pe.wait_ge(misc_free, used)
                bank = misc.fill()
                for v in range(2):
                    t = 2 * half + v
                    last = nc.tensor.matmul(bank[:, v * QKV:(v + 1) * QKV], xnT[:, t * P:(t + 1) * P], w_qkv[:, :],
                                            start=(v == 0), stop=True, skip_group_check=True)
                last.then_inc(misc_full, 1)

            def k_transpose(misc, b, which):
                pe.wait_ge(rows_ready, b * 9 + 9)
                bank = misc.fill()[:, :].bitcast(bf16)
                for v in range(2):
                    for t in range(T):
                        at = (v * T + t) * P
                        last = nc.tensor.transpose(bank[:, at:at + P],
                                                   k_rows[:, t, 2 * which + v, :, :, :].rearrange("p v r d -> p (v r d)"),
                                                   ident_b[:, :])
                last.then_inc(misc_full, 1)

            def q_transpose(misc, t):
                bank = misc.fill()[:, :].bitcast(bf16)
                for j in range(HEADS // 2):
                    last = nc.tensor.transpose(bank[:, j * P:(j + 1) * P],
                                               q_rows[:, t, 2 * j:2 * j + 2, :, :].rearrange("p h r d -> p (h r d)"),
                                               ident_b[:, :])
                last.then_inc(misc_full, 1)

            def expert_of(n, ahead):
                return pe.value_load(tile_e[0:1, bass.ds(n + ahead, 1)], min_val=0, max_val=E - 1)

            def slot(misc, b, par, s, before_it):
                n, k = slot_number(b, s), par * PER_BATCH + s
                e_out = expert_of(n, 0)
                bank = misc.fill()
                pe.wait_ge(xs_loaded[k % X_RING], rounds(b, par, X_RING) + 16 * (k // X_RING + 1))
                nc.tensor.transpose(bank[:, 0:P], xs[k % X_RING], ident[:, :])
                pe.wait_ge(hid_free, HID_CREDIT + 1 - (LAG - H_LAG) + n)
                for c in range(FC):
                    last = nc.tensor.matmul(bank[:, P:2 * P], hT[(k - LAG) % T_RING][:, c * P:(c + 1) * P],
                                            w2_sb[:, bass.ds(e_out * F + c * P, P)], start=False, stop=(c == FC - 1),
                                            skip_group_check=True)
                last.then_inc(misc_full, 1)
                m = k - H_LAG
                pe.wait_ge(w1_loaded[m % W_RING], rounds(b, par, W_RING) + 16 * (m // W_RING + 1 + (m % W_RING >= W_RING - H_LAG)))
                pe.wait_ge(misc_free, before_it)
                pe.wait_ge(hid_free, HID_CREDIT + n)
                for c in range(FC):
                    last = nc.tensor.matmul(ps_hid[:, c * P:(c + 1) * P], w1_t[m % W_RING][:, c * P:(c + 1) * P],
                                            xsT[m % T_RING], start=(c == 0), stop=True, skip_group_check=True)
                last.then_inc(hid_full, 1)

            misc = Misc(pe, None)
            x_transpose(misc, 0)
            for half in range(2):
                qkv(misc, half, 1)
            for which in range(2):
                k_transpose(misc, 0, which)
            for t in range(T):
                q_transpose(misc, t)

            pe.wait_ge(misc_free, 9)
            for g, k in EARLY:
                scores(0, g, 0, k)

            pe.wait_ge(onehot_ready, PICKS)
            bank = misc.fill()
            for e in range(E):
                last = nc.tensor.matmul(bank[:, e:e + 1], oh_b[:, e, :], ones_b[:, :], start=(e == 0), stop=True,
                                        skip_group_check=True)
            last.then_inc(misc_full, 1)
            pe.wait_ge(misc_free, 10)
            bank = misc.fill()
            for e in range(E):
                last = nc.tensor.matmul(bank[:, e:e + 1], tot_b[:, e, :], ones_b[:, :], start=(e == 0), stop=True,
                                        skip_group_check=True)
            last.then_inc(misc_full, 1)
            half_e = E // 2
            for half in range(2):
                bank = misc.fill()
                nc.tensor.matmul(bank[:, :].rearrange("p (e c) -> p e c", e=half_e), before[:, :],
                                 oh_b[:, half * half_e:(half + 1) * half_e, :], start=True, stop=False, skip_group_check=True)
                for v in range(half_e):
                    last = nc.tensor.matmul(bank[:, v * P:(v + 1) * P], tot_b[:, half * half_e + v, :], before[:, :],
                                            start=False, stop=True, skip_group_check=True)
                last.then_inc(misc_full, 1)

            def body(b, par):
                misc = Misc(pe, b, par)
                first, last, moe, comb = kind(b)
                if not first:
                    pe.wait_ge(kq_ready, b)
                s, ends = 0, [0, 0]
                for part, *a in order(first, last, moe, comb):
                    if part == "scores":
                        if not (first and (a[0], a[1]) in EARLY):
                            scores(b, a[0], par, a[1])
                    elif part == "pv":
                        pv(b, a[0], par, a[1])
                    elif part == "pv_prev":
                        pv(b - 1, a[0], 1 - par, a[1])
                    elif part in ("y_transpose", "y_transpose_prev"):
                        y_transpose(misc, b - (part != "y_transpose"), a[0])
                        if part == "y_transpose_prev":
                            y_used = misc.base + misc.k
                    elif part == "y_tok_transpose_prev":
                        y_tok_transpose(misc, y_used)
                        yT_used = misc.base + misc.k
                    elif part == "out_proj_prev":
                        out_proj(misc, yT_used)
                    elif part == "x_transpose":
                        x_transpose(misc, b + 1)
                        x_used = misc.base + misc.k
                    elif part == "qkv":
                        qkv(misc, a[0], x_used)
                    elif part == "k_transpose":
                        k_transpose(misc, b + 1, a[0])
                    elif part == "q_transpose":
                        q_transpose(misc, a[0])
                    elif part == "slot":
                        slot(misc, b, par, s, misc.base + ends[-2])
                        ends.append(misc.k)
                        s += 1
            run = batches(body)
            next(run)
            pe.wait_ge(ew_loaded, 16)
            pe.wait_ge(space_clear, 1)
            moe_batches(pe, body)
            next(run)
            b = BATCH - 1
            misc = Misc(pe, b)
            misc.k = LAST_USES
            for half in range(2):
                pv(b, KV - 1, 1, half)
            y_transpose(misc, b, 2)
            y_transpose(misc, b, 3)
            y_tok_transpose(misc, misc.base + misc.k)
            out_proj(misc, misc.base + misc.k)

        @block.vector
        def _(dve):
            V = nc.vector

            V.memset(zero_rows, 0.0).then_inc(zero_made, 1)

            def newton(sem_, base, a, y, tmp, parts=(0, 1)):
                def step(n):
                    for k, ins in enumerate((lambda: V.tensor_tensor(tmp, y, y, ALU.mult),
                                             lambda: V.scalar_tensor_tensor(tmp, tmp, -0.5, a, ALU.mult, ALU.mult),
                                             lambda: V.scalar_tensor_tensor(y, tmp, 1.5, y, ALU.add, ALU.mult))):
                        dve.wait_ge(sem_, base + 3 * n + k + 2)
                        ins().then_inc(sem_, 1)
                if 0 in parts:
                    V.tensor_scalar(tmp.bitcast(i32), a.bitcast(i32), 1, None, ALU.logical_shift_right).then_inc(sem_, 1)
                    dve.wait_ge(sem_, base + 1)
                    V.tensor_scalar(y.bitcast(i32), tmp.bitcast(i32), -1.0, float(0x5f3759df), ALU.mult, ALU.add).then_inc(sem_, 1)
                    step(0)
                if 1 in parts:
                    step(1)
                    step(2)

            def row_stats(b, q, loads):
                if not isinstance(b, int) or b >= 2:
                    dve.wait_ge(aggr_done, b * T - T)
                dve.wait_ge(x_loaded[q], 16 * loads)
                for t in range(T):
                    V.bn_stats(stats[q % 2][:, t, :], x_res[:, bass.ds(b * (T * D) + t * D, D)]).then_inc(stat_done, 1)

            def mean_var(b, par):
                if not isinstance(b, int) or b >= 2:
                    dve.wait_ge(mv_ready, b - 1)
                dve.wait_ge(stat_done, b * T + T)
                dve.sem_inc(dve_tick, 1)
                for t in range(T):
                    V.bn_aggr(mv_tmp[par][:, t, :], stats[par][:, t, :]).then_inc(aggr_done, 1)

            def keep(b, par):
                dve.wait_ge(aggr_done, b * T + T)
                V.tensor_copy(mv[:, bass.ds(b * T, T), :], mv_tmp[par][:, :, :]).then_inc(mv_ready, 1)

            for b in range(X_LOADS):
                row_stats(b, b, 1)
                if b >= 1:
                    mean_var(b - 1, (b - 1) % 2)
                if b >= 2:
                    keep(b - 2, b % 2)
            with dve.Fori(1, BATCH // X_LOADS) as i:
                for q in range(X_LOADS):
                    b = i * X_LOADS + q
                    row_stats(b, q, i + 1)
                    mean_var(b - 1, (q - 1) % 2)
                    keep(b - 2, q % 2)
            mean_var(BATCH - 1, 1)
            keep(BATCH - 2, 0)
            keep(BATCH - 1, 1)
            dve.wait_ge(mv_ready, BATCH)
            V.tensor_scalar(ve, mv[:, :, 1], EPS, None, ALU.add).then_inc(ln_chain, 1)
            dve.wait_ge(ln_chain, 1)
            newton(ln_chain, 1, ve, rstd[:, :], nr_tmp)
            dve.wait_ge(ln_chain, 1 + NEWTON)

            def normalise(b, dst, done):
                for t in range(T):
                    V.tensor_scalar(dst[:, t, :], x_res[:, bass.ds(b * (T * D) + t * D, D)],
                                    mv[:, bass.ds(b * T + t, 1), 0], rstd[:, bass.ds(b * T + t, 1)],
                                    ALU.subtract, ALU.mult).then_inc(done, 1)

            def take_logits(b, par):
                dve.wait_ge(pro_lg_full, b + 1)
                V.tensor_tensor(lg[:, bass.ds(b * T, T), :],
                                ps_score[par][:, 512:512 + T * E].rearrange("p (t e) -> p t e", e=E),
                                br_sb[:, :].unsqueeze(1).broadcast_to([P, T, E]), ALU.add).then_inc(pro_lg_done, 1)
            dve.wait_ge(w_loaded, 16 * 12)
            dve.wait_ge(consts_made, 14)
            normalise(0, pro_xn_buf[0], pro_xn)
            normalise(1, pro_xn_buf[1], pro_xn)
            with dve.Fori(1, BATCH // 2) as i:
                for par in range(2):
                    b = i * 2 + par
                    dve.wait_ge(pro_xT_full, b - 1)
                    dve.wait_ge(pro_copied, b - 1)
                    normalise(b, pro_xn_buf[par], pro_xn)
                    take_logits(b - 2, par)
            take_logits(BATCH - 2, 0)
            take_logits(BATCH - 1, 1)

            def take(misc, dst):
                bank = misc.drain()
                V.tensor_copy(dst, bank[:, :]).then_inc(misc_free, 1)

            def take_qkv(misc, par, half):
                bank = misc.drain()[:, 0:2 * QKV].rearrange("p (u c) -> p u c", u=2)
                V.tensor_copy(qk[:, 2 * half:2 * half + 2, :, :].rearrange("p u h d -> p u (h d)"),
                              bank[:, :, 0:QK]).then_inc(qk_ready, 1)
                V.tensor_copy(v_aug[par][:, 2 * half:2 * half + 2, :, 0:HD],
                              bank[:, :, QK:QKV].rearrange("p u (g d) -> p u g d", g=KV)).then_inc(misc_free, 1)

            def qk_square(b):
                dve.wait_ge(qk_ready, 2 * b + 2)
                V.tensor_tensor(qk_a[:, :, :, :], qk[:, :, :, :], qk[:, :, :, :], ALU.mult).then_inc(sq_ready, 1)
                dve.wait_ge(sq_ready, b + 1)
                V.tensor_reduce(ms[:, :], qk_a[:, :, :, :].rearrange("p t h d -> p (t h) d"), X, ALU.add).then_inc(ms_ready, 1)
                dve.wait_ge(ms_ready, 2 * b + 1)
                V.tensor_scalar(ms[:, :], ms[:, :], 1.0 / HD, EPS, ALU.mult, ALU.add).then_inc(ms_ready, 1)

            def qk_root(b, parts):
                dve.wait_ge(ms_ready, 2 * b + 2)
                newton(rms_chain, b * NEWTON, ms[:, :], rms[:, :], rms_tmp[:, :], parts)

            by_head = [P, T, HEADS + KV, HD]

            def qk_scale(b):
                dve.wait_ge(rms_chain, b * NEWTON + NEWTON)
                v = qk[:, :, :, :].rearrange("p t h d -> p (t h) d")
                V.tensor_tensor(v, v, rms[:, :].unsqueeze(2).broadcast_to([P, T * (HEADS + KV), HD]), ALU.mult).then_inc(qkn_ready, 1)
                dve.wait_ge(qkn_ready, b + 1)
                V.tensor_tensor(qk_a[:, :, :, :], qk[:, :, :, :], cos2[:, :, :].unsqueeze(2).broadcast_to(by_head),
                                ALU.mult).then_inc(rope_step, 1)

            def qk_rotate(b):
                for half in range(2):
                    o, s = HD // 2 * half, HD // 2 * (1 - half)
                    V.tensor_tensor(qk_b[:, :, :, o:o + HD // 2], qk[:, :, :, s:s + HD // 2],
                                    sin2[:, :, o:o + HD // 2].unsqueeze(2).broadcast_to([P, T, HEADS + KV, HD // 2]),
                                    ALU.mult).then_inc(rope_step, 1)
                dve.wait_ge(rope_step, 3 * b + 3)
                V.tensor_tensor(qk_a[:, :, :, :], qk_a[:, :, :, :], qk_b[:, :, :, :], ALU.add).then_inc(rope_ready, 1)

            qk_rms = (qk_square, lambda b: qk_root(b, (0,)), lambda b: qk_root(b, (1,)), qk_scale, qk_rotate)

            def split_first(b):
                dve.wait_ge(rope_ready, b + 1)
                V.tensor_copy(parts[0][:, :, :, :], qk_a[:, :, :, :]).then_inc(split_ready, 1)
                dve.wait_ge(split_ready, 4 * b + 1)
                V.tensor_tensor(qk_b[:, :, :, :], qk_a[:, :, :, :], parts[0][:, :, :, :], ALU.subtract).then_inc(split_ready, 1)

            def split_rest(b):
                dve.wait_ge(split_ready, 4 * b + 2)
                V.tensor_copy(parts[1][:, :, :, :], qk_b[:, :, :, :]).then_inc(split_ready, 1)
                dve.wait_ge(split_ready, 4 * b + 3)
                V.tensor_tensor(parts[2][:, :, :, :], qk_b[:, :, :, :], parts[1][:, :, :, :], ALU.subtract).then_inc(split_ready, 1)

            def lay_rows(b, which):
                dve.wait_ge(split_ready, 4 * b + (4 if 2 in which else 3))
                for n in which:
                    part = parts[n]
                    c = len(range(n, TERMS, 3))
                    for var in range(2):
                        V.tensor_copy(k_rows[:, :, :, var, n:TERMS:3, :],
                                      part[:, :, HEADS:HEADS + KV, :].unsqueeze(3).broadcast_to([P, T, KV, c, HD])).then_inc(rows_ready, 1)
                    c = min(3, TERMS - 3 * n)
                    V.tensor_copy(q_rows[:, :, :, 3 * n:3 * n + c, :],
                                  part[:, :, 0:HEADS, :].unsqueeze(3).broadcast_to([P, T, HEADS, c, HD])).then_inc(rows_ready, 1)

            split = (split_first, split_rest, lambda b: lay_rows(b, (0, 1)), lambda b: lay_rows(b, (2,)))

            def take_k(misc, par, which):
                bank = misc.drain()[:, :].bitcast(bf16).rearrange("p (u c) -> p u c", u=2)
                V.tensor_copy(kT[par][0:ROWS, 2 * which:2 * which + 2, 0, :], bank[0:ROWS]).then_inc(kT_half, 1)
                V.tensor_copy(kT[par][ROWS:P, 2 * which:2 * which + 2, 1, :], bank[ROWS:P]).then_inc(misc_free, 1)

            def take_q(misc, par, t):
                bank = misc.drain()[:, :].bitcast(bf16).rearrange("p (j c) -> p j c", c=P)
                V.tensor_copy(qT[par][:, :, t * P:(t + 1) * P], bank).then_inc(misc_free, 1)

            def take_y(b, g):
                dve.wait_ge(pv_done, b * 4 + (g + 1))
                V.tensor_copy(y_raw[g % 2][:, :], ps_y[:, :]).then_inc(y_free, 1)

            def normalise_y(misc, b, g):
                bank = misc.drain()[:, :].rearrange("p (th c) -> p th c", c=32)
                V.reciprocal(den[g % 2][:, :], bank[:, :, HD]).then_inc(den_ready, 1)
                dve.wait_ge(den_ready, b * 4 + (g + 1))
                V.tensor_tensor(
                    y_tok[:, :, g * REP * HD:(g + 1) * REP * HD].rearrange("p t (h d) -> p t h d", d=HD),
                    bank[:, :, 0:HD].rearrange("p (t h) d -> p t h d", t=T),
                    den[g % 2][:, :].rearrange("p (t h) -> p t h", t=T).unsqueeze(3).broadcast_to([P, T, REP, HD]),
                    ALU.mult).then_inc(misc_free, 1)

            def add_out(misc, b):
                bank = misc.drain()
                v = x_res[:, bass.ds(b * (T * D), T * D)]
                V.tensor_tensor(v, v, bank[:, :], ALU.add).then_inc(misc_free, 1)
                dve.wait_ge(misc_free, misc.base + misc.k)
                v = v.rearrange("p (t d) -> p t d", t=T)
                V.tensor_tensor(v, v, gb[:, 1, :].unsqueeze(1).broadcast_to([P, T, D]), ALU.add).then_inc(beta_added, 1)

            def expert_of(n, ahead):
                return dve.value_load(tile_e[0:1, bass.ds(n + ahead, 1)], min_val=0, max_val=E - 1)

            def slot(misc, b, par, s):
                n, k = slot_number(b, s), par * PER_BATCH + s
                e_out = expert_of(n, 0)
                bank = misc.drain()
                V.tensor_copy(xsT[k % T_RING], bank[:, 0:P])
                dve.wait_ge(o_stored[k % O_RING], rounds(b, par, O_RING) + 16 * (k // O_RING + 1))
                V.tensor_tensor(o_row[k % O_RING], bank[:, P:2 * P], b2_sb[:, bass.ds(e_out * D, D)], ALU.add).then_inc(misc_free, 1)
                dve.wait_ge(misc_free, misc.base + misc.k)
                V.tensor_tensor(o_row[k % O_RING], o_row[k % O_RING], xs[(k - LAG) % X_RING], ALU.add).then_inc(o_ready, 1)

            def sum_picks(c):
                dve.wait_ge(scaled, c + 1)
                tiles = range(c * T, (c + 1) * T)
                for t in tiles:
                    last = V.scalar_tensor_tensor(u[:, t, :], picked[c % 2][:, t % T, 0, :], weight[:, 0, t:t + 1],
                                                  picked[c % 2][:, t % T, 1, :], ALU.mult, ALU.add)
                last.then_inc(summed, 1)
                dve.wait_ge(summed, c + 1)
                for t in tiles:
                    last = V.bn_stats(stats[0][:, t % T, :], u[:, t, :])
                last.then_inc(c_stats, 1)
                dve.wait_ge(c_stats, c + 1)
                for t in tiles:
                    last = V.bn_aggr(c_mv[:, t, :], stats[0][:, t % T, :])
                last.then_inc(c_mv_ready, 1)
                dve.wait_ge(c_mv_ready, c + 1)

            def group_root(i):
                v = slice(GROUPS[i][0] * T, (GROUPS[i][-1] + 1) * T)
                base = i * (NEWTON + 1)
                V.tensor_scalar(c_ve[:, v], c_mv[:, v, 1], EPS, None, ALU.add).then_inc(c_chain, 1)
                dve.wait_ge(c_chain, base + 1)
                newton(c_chain, base + 1, c_ve[:, v], c_rstd[:, v], c_tmp[:, v])
                dve.wait_ge(c_chain, base + 1 + NEWTON)
                V.scalar_tensor_tensor(c_shift[:, v], c_mv[:, v, 0], -1.0, c_rstd[:, v], ALU.mult, ALU.mult).then_inc(c_rstd_ready, 1)

            def finish(c):
                dve.wait_ge(centred, c + 1)
                v = u[:, c * T:(c + 1) * T, :]
                V.tensor_tensor(v, v, gb[:, 0, :].unsqueeze(1).broadcast_to([P, T, D]), ALU.mult).then_inc(fin_chain, 1)
                dve.wait_ge(fin_chain, c + 1)
                dve.wait_ge(beta_added, c + 1)
                V.tensor_tensor(v, v, x_res[:, c * T * D:(c + 1) * T * D].rearrange("p (t d) -> p t d", t=T), ALU.add).then_inc(combined, 1)

            misc = Misc(dve, None)
            dve.wait_ge(pro_xT_full, BATCH)
            dve.wait_ge(pro_copied, BATCH)
            normalise(0, xn, xn_ready)
            take(misc, xnT[:, :])
            take_qkv(misc, 0, 0)
            take_qkv(misc, 0, 1)
            for stage in qk_rms + split:
                stage(0)
            take_k(misc, 0, 0)
            take_k(misc, 0, 1)
            for t in range(T):
                take_q(misc, 0, t)

            steps = [0]

            def link(ins):
                ins.then_inc(route, 1)
                steps[0] += 1
                dve.wait_ge(route, steps[0])
            dve.wait_ge(pro_lg_done, BATCH)
            by_e = [P, TILES, E]
            rev = rev_e[:, :].unsqueeze(1).broadcast_to(by_e)
            logits = lg
            for j in range(PICKS):
                link(V.tensor_reduce(m12[:, j, :], logits, X, ALU.max))
                link(V.tensor_tensor(r_tmp, logits, m12[:, j, :].unsqueeze(2).broadcast_to(by_e), ALU.is_equal))
                link(V.tensor_tensor(r_tmp, r_tmp, rev, ALU.mult))
                link(V.tensor_reduce(r_idx, r_tmp, X, ALU.max))
                link(V.tensor_tensor(oh[:, j, :, :], rev, r_idx.unsqueeze(2).broadcast_to(by_e), ALU.is_equal))
                V.tensor_copy(oh_b[:, :, j * TILES:(j + 1) * TILES], oh[:, j, :, :].rearrange("p t e -> p e t")).then_inc(onehot_ready, 1)
                if j == 0:
                    link(V.scalar_tensor_tensor(lg2.rearrange("p t e -> p (t e)"), oh[:, 0, :, :].rearrange("p t e -> p (t e)"),
                                                -1e30, lg.rearrange("p t e -> p (t e)"), ALU.mult, ALU.add))
                    logits = lg2
            V.tensor_tensor(gap, m12[:, 1, :], m12[:, 0, :], ALU.subtract).then_inc(gap_ready, 1)
            bank = misc.drain()
            V.tensor_copy(tot_b, bank[:, 0:E].unsqueeze(2).broadcast_to([P, E, P])).then_inc(misc_free, 1)
            bank = misc.drain()
            V.tensor_scalar(cnt_i, bank[:, 0:E], float(P - 1), None, ALU.add).then_inc(misc_free, 1)
            dve.wait_ge(misc_free, 11)
            link(V.tensor_scalar(cnt_i, cnt_i, 7, None, ALU.logical_shift_right))
            link(V.tensor_copy(nt, cnt_i))
            a, b_ = nt, inc1
            for sh in (1, 2, 4):
                link(V.tensor_copy(b_[:, 0:sh], a[:, 0:sh]))
                link(V.tensor_tensor(b_[:, sh:E], a[:, sh:E], a[:, 0:E - sh], ALU.add))
                a, b_ = b_, (inc2 if b_ is inc1 else inc1)
            incl = a
            link(V.tensor_tensor(start, incl, nt, ALU.subtract))
            link(V.tensor_scalar(start, start, float(P), None, ALU.mult))
            for half in range(2):
                bank = misc.drain()
                hv = slice(half * E // 2, (half + 1) * E // 2)
                V.tensor_tensor(rank[:, hv, :], bank[:, :].rearrange("p (e c) -> p e c", e=E // 2),
                                start[:, hv].unsqueeze(2).broadcast_to([P, E // 2, P]), ALU.add).then_inc(misc_free, 1)
            dve.wait_ge(misc_free, PRE)
            link(V.tensor_tensor(rank, rank, oh_b, ALU.mult))
            link(V.tensor_reduce(slot_f, rank.rearrange("p e c -> p c e"), X, ALU.add))
            V.tensor_copy(slot_i[:, :, :].rearrange("p j t -> p (j t)"), slot_f).then_inc(slots_ready, 1)
            link(V.tensor_scalar(oslot_i[:, :, :].rearrange("p j t -> p (j t)"), slot_f, float(LAG * P), None, ALU.add))
            n_all = E_TILES
            link(V.tensor_tensor(cmp, slot_nr[:, :].unsqueeze(1).broadcast_to([1, E - 1, n_all]),
                                 incl[0:1, 0:E - 1].unsqueeze(2).broadcast_to([1, E - 1, n_all]), ALU.is_ge))
            link(V.tensor_reduce(tile_f, cmp.rearrange("p e n -> p n e"), X, ALU.add))
            V.tensor_copy(tile_e[:, :], tile_f).then_inc(tile_e_ready, 1)

            def body(b, par):
                misc = Misc(dve, b, par)
                first, last, moe, comb = kind(b)
                if not moe and b == FIRST_MOE - 1:
                    V.memset(space[:, :], 0.0).then_inc(space_clear, 1)
                    dve.wait_ge(space_clear, 1)
                s = 0
                for part, *a in order(first, last, moe, comb):
                    if part in ("pv", "pv_prev"):
                        if a[1] == 1:
                            take_y(b - (part != "pv"), a[0])
                    elif part in ("y_transpose", "y_transpose_prev"):
                        normalise_y(misc, b - (part != "y_transpose"), a[0])
                    elif part == "y_tok_transpose_prev":
                        take(misc, yT[:, :])
                    elif part == "out_proj_prev":
                        add_out(misc, b - 1)
                    elif part == "normalise_x":
                        normalise(b + 1, xn, xn_ready)
                    elif part == "x_transpose":
                        take(misc, xnT[:, :])
                    elif part == "qkv":
                        take_qkv(misc, 1 - par, a[0])
                    elif part == "qk_rms":
                        qk_rms[a[0]](b + 1)
                    elif part == "split":
                        split[a[0]](b + 1)
                    elif part == "k_transpose":
                        take_k(misc, 1 - par, a[0])
                    elif part == "q_transpose":
                        take_q(misc, 1 - par, a[0])
                        if a[0] == T - 1:
                            dve.wait_ge(misc_free, misc.base + misc.k)
                            dve.sem_inc(kq_ready, 1)
                    elif part == "slot":
                        slot(misc, b, par, s)
                        s += 1
                    elif part == "finish":
                        for c in FINISH.get((b - LAST_MOE) * KV + a[0], ()):
                            finish(c)
                    elif part == "sum":
                        c = (b - LAST_MOE) * KV + a[0] - 1
                        if c >= 0:
                            sum_picks(c)
                        for i, group in enumerate(GROUPS):
                            if group[-1] == c:
                                group_root(i)
                    if first and (part, *a) == ("pv", 0, 1):
                        dve.wait_ge(gap_exp, 1)
                        link(V.tensor_scalar(weight[:, 0, :], gap_e, 1.0, None, ALU.add))
                        link(V.reciprocal(weight[:, 0, :], weight[:, 0, :]))
                        link(V.tensor_tensor(weight[:, 1, :], gap_e, weight[:, 0, :], ALU.mult))
            run = batches(body)
            next(run)
            moe_batches(dve, body)
            next(run)
            b = BATCH - 1
            misc = Misc(dve, b)
            misc.k = LAST_USES
            sum_picks(BATCH - 1)
            take_y(b, 3)
            group_root(len(GROUPS) - 1)
            normalise_y(misc, b, 2)
            normalise_y(misc, b, 3)
            take(misc, yT[:, :])
            add_out(misc, b)
            for c in GROUPS[-1]:
                finish(c)


def kernel(**inputs):
    import concourse.bacc as bacc
    from concourse.bass_utils import run_bass_kernel_spmd

    nc = bacc.Bacc("TRN2", target_bir_lowering=False, num_devices=1)
    get = {n: np.asarray(a) for n, a in inputs.items()}
    inv_freq = (1.0 / THETA ** (np.arange(0, HD, 2, dtype=np.float32) / np.float32(HD))).astype(np.float32)
    angle = np.arange(SEQ, dtype=np.float32)[:, None] * inv_freq[None, :]
    cos, sin = np.cos(angle), np.sin(angle)
    rope = np.stack([np.concatenate([cos, cos], 1), np.concatenate([-sin, sin], 1)])
    laid = {
        "x": get["L0_attn_x"],
        "w_q": get["L0_attn_w_q"], "w_k": get["L0_attn_w_k"], "w_v": get["L0_attn_w_v"], "w_o": get["L0_attn_w_o"],
        "b1t": get["L0_ffn_b1"].reshape(E * FC, P).T,
        "w1t": get["L0_ffn_W1"].transpose(2, 0, 1).reshape(D, E * F),
        "w2t": get["L0_ffn_W2"].transpose(0, 2, 1).reshape(E * FC, P, D).transpose(1, 0, 2),
        "wrt": get["L0_ffn_Wr"].T,
        "br": get["L0_ffn_br"], "b2": get["L0_ffn_b2"], "gamma": get["L0_ffn_gamma"], "beta": get["L0_ffn_beta"],
        "rope": rope.astype(np.float32),
    }
    laid = {n: np.ascontiguousarray(a) for n, a in laid.items()}
    args = {n: nc.dram_tensor(f"in_{n}", a.shape, mybir.dt.from_np(a.dtype), kind="ExternalInput").ap() for n, a in laid.items()}
    out = nc.dram_tensor("out_0", (BATCH, SEQ, D), mybir.dt.float32, kind="ExternalOutput").ap()
    build_program(nc, out=out, **args)
    r = run_bass_kernel_spmd(nc, [{f"in_{n}": a for n, a in laid.items()}], core_ids=[0])
    return r.results[0]["out_0"]
```
